# Optimizing a Trainium2 kernel written in Bass

```python
import numpy as np
import jax
import jax.numpy as jnp

def _softmax(x, axis=-1):
    return jax.nn.softmax(x, axis=axis)

def _gelu(x):
    return jax.nn.gelu(x, approximate=True)

def _silu(x):
    return jax.nn.silu(x)

def _sigmoid(x):
    return jax.nn.sigmoid(x)

def _layernorm(x, axis=-1, eps=1e-05):
    m = jnp.mean(x, axis=axis, keepdims=True)
    v = jnp.var(x, axis=axis, keepdims=True)
    return (x - m) / jnp.sqrt(v + eps)

def _scatter_add(tgt, idx, src, axis=0):
    return tgt.at[idx].add(src)

def _segment_sum(src, seg, n):
    return jax.ops.segment_sum(src, seg, n)
kernel_name = 'mk_conv_attn_hybrid_d2_conv_nhwc256_r4_ff904c'

def setup_inputs(seed: int=0):
    np.random.seed(seed)
    _w = jnp.asarray

    def _rec_inputs():
        import jax
        import jax.numpy as jnp
        _gk = jax.random.key(seed)
        x = -0.0005207 + 1.001 * jax.random.normal(jax.random.fold_in(_gk, 1), (2, 16, 16, 64), jnp.float32)
        return x
    x = _rec_inputs()

    def _L0_conv_setup():
        import jax, jax.numpy as jnp
        import numpy as np
        B, H, W = (2, 16, 16)
        D_MODEL, D_STATE, DT_RANK = (64, 16, 16)
        D_INNER = 2 * D_MODEL

        def _selective_scan(u, delta, A, Bm, Cm, Dv):

            def step(h, inp):
                dt, bt, ct, ut = inp
                h = jnp.exp(dt[..., None] * A) * h + (dt * ut)[..., None] * bt[:, None, :]
                return (h, jnp.einsum('bdn,bn->bd', h, ct))
            h0 = jnp.zeros(u.shape[:2] + (A.shape[1],), u.dtype)
            xs = (jnp.moveaxis(delta, 2, 0), jnp.moveaxis(Bm, 2, 0), jnp.moveaxis(Cm, 2, 0), jnp.moveaxis(u, 2, 0))
            _, ys = jax.lax.scan(step, h0, xs)
            return jnp.moveaxis(ys, 0, 2) + Dv[None, :, None] * u

        def _forward(x, in_proj_w, conv_w, conv_b, xproj_w, dt_w, dt_b, A_logs, Ds, out_proj_w):
            b, h, w, _ = x.shape
            n, r = (D_STATE, DT_RANK)
            l = h * w
            xz = x @ in_proj_w
            xi, z = jnp.split(xz, 2, axis=-1)
            xc = jnp.transpose(xi, (0, 3, 1, 2))
            xc = jax.lax.conv_general_dilated(xc, conv_w, (1, 1), ((1, 1), (1, 1)), dimension_numbers=('NCHW', 'OIHW', 'NCHW'))
            xc = jax.nn.silu(xc + conv_b[None, :, None, None])
            x_dbl = jnp.einsum('bchw,oc->bohw', xc, xproj_w)
            half = x_dbl.shape[1] // 2
            hw_flat = x_dbl[:, :half].reshape(b, half, l)
            wh_flat = jnp.transpose(x_dbl[:, half:], (0, 1, 3, 2)).reshape(b, half, l)

            def split_params(flat):
                dts, bc = (flat[:, :2 * r], flat[:, 2 * r:])
                return ((dts[:, :r], dts[:, r:]), (bc[:, :n], bc[:, n:2 * n]), (bc[:, 2 * n:3 * n], bc[:, 3 * n:]))
            (hd1, hd2), (hb1, hb2), (hc1, hc2) = split_params(hw_flat)
            (wd1, wd2), (wb1, wb2), (wc1, wc2) = split_params(wh_flat)
            hw_x = xc.reshape(b, -1, l)
            wh_x = jnp.transpose(xc, (0, 1, 3, 2)).reshape(b, -1, l)
            xs = jnp.stack([hw_x, hw_x[:, ::-1], wh_x, wh_x[:, ::-1]])
            dt_stack = jnp.stack([hd1, hd2, wd1, wd2])
            Bst = jnp.stack([hb1, hb2, wb1, wb2])
            Cst = jnp.stack([hc1, hc2, wc1, wc2])
            dts = jnp.einsum('kbrl,kdr->kbdl', dt_stack, dt_w)
            delta = jax.nn.softplus(dts + dt_b[:, None, :, None])
            A = -jnp.exp(A_logs)
            ys = jax.vmap(_selective_scan)(xs, delta, A, Bst, Cst, Ds)
            y = ys.sum(0)
            y = jnp.transpose(y, (0, 2, 1)).reshape(b, h, w, -1)
            y = y * jax.nn.silu(z)
            return y @ out_proj_w
        key = jax.random.key(seed)
        ks = jax.random.split(key, 8)
        f = lambda k, shape, s=0.02: jax.random.normal(k, shape, dtype=jnp.float32) * s
        x = jax.random.normal(ks[0], (B, H, W, D_MODEL), dtype=jnp.float32)
        in_proj_w = f(ks[1], (D_MODEL, 2 * D_INNER))
        conv_w = f(ks[2], (D_INNER, D_INNER, 3, 3))
        conv_b = jnp.zeros((D_INNER,), jnp.float32)
        xproj_w = f(ks[3], (4 * (DT_RANK + 2 * D_STATE), D_INNER))
        std = DT_RANK ** (-0.5)
        dt_w = jax.random.uniform(ks[4], (4, D_INNER, DT_RANK), jnp.float32, -std, std)
        dt = jnp.exp(jax.random.uniform(ks[5], (4, D_INNER), jnp.float32) * (np.log(0.1) - np.log(0.001)) + np.log(0.001)).clip(0.0001)
        dt_b = dt + jnp.log(-jnp.expm1(-dt))
        A_logs = jnp.log(jnp.tile(jnp.arange(1, D_STATE + 1, dtype=jnp.float32)[None, None, :], (4, D_INNER, 1)))
        Ds = jnp.ones((4, D_INNER), jnp.float32)
        out_proj_w = f(ks[6], (D_INNER, D_MODEL))
        return dict(x=x, in_proj_w=in_proj_w, conv_w=conv_w, conv_b=conv_b, xproj_w=xproj_w, dt_w=dt_w, dt_b=dt_b, A_logs=A_logs, Ds=Ds, out_proj_w=out_proj_w)
    _L0_conv_all = _L0_conv_setup()
    _L0_conv_in = {k: v for k, v in _L0_conv_all.items() if k in ('in_proj_w', 'conv_w', 'conv_b', 'xproj_w', 'dt_w', 'dt_b', 'A_logs', 'Ds', 'out_proj_w')}
    del _L0_conv_all

    def _L1_attn_setup():
        import jax, jax.numpy as jnp
        import numpy as np
        W = 3
        key = jax.random.key(seed)
        ks = jax.random.split(key, 7)
        B, N, D = (8, 1024, 64)
        s = 1.0 / np.sqrt(D)
        return {'x': jax.random.normal(ks[0], (B, N, D), jnp.float32), 'Wq': jax.random.normal(ks[1], (D, D), jnp.float32) * s, 'bq': jax.random.normal(ks[2], (D,), jnp.float32) * 0.01, 'Wk': jax.random.normal(ks[3], (D, D), jnp.float32) * s, 'bk': jax.random.normal(ks[4], (D,), jnp.float32) * 0.01, 'Wv': jax.random.normal(ks[5], (D, D), jnp.float32) * s, 'bv': jax.random.normal(ks[6], (D,), jnp.float32) * 0.01}
    _L1_attn_all = _L1_attn_setup()
    _L1_attn_in = {k: v for k, v in _L1_attn_all.items() if k in ('Wq', 'bq', 'Wk', 'bk', 'Wv', 'bv')}
    del _L1_attn_all

    def _L1_ffn_setup():
        import jax, jax.numpy as jnp
        import numpy as np
        N_EXPERTS = 8
        TOP_K = 2
        key = jax.random.key(seed)
        ks = jax.random.split(key, 5)
        B, T, C, E, H = (8, 512, 64, 8, 682)
        scale = 1.0 / np.sqrt(C)
        return {'x': jax.random.normal(ks[0], (B, T, C), dtype=jnp.float32), 'router_w': jax.random.normal(ks[1], (E, C), dtype=jnp.float32) * scale, 'w1': jax.random.normal(ks[2], (E, H, C), dtype=jnp.float32) * scale, 'w2': jax.random.normal(ks[3], (E, C, H), dtype=jnp.float32) * (1.0 / np.sqrt(H)), 'w3': jax.random.normal(ks[4], (E, H, C), dtype=jnp.float32) * scale}
    _L1_ffn_all = _L1_ffn_setup()
    _L1_ffn_in = {k: v for k, v in _L1_ffn_all.items() if k in ('router_w', 'w1', 'w2', 'w3')}
    del _L1_ffn_all
    return {'x': x, 'L0_conv_in_proj_w': _L0_conv_in['in_proj_w'], 'L0_conv_conv_w': _L0_conv_in['conv_w'], 'L0_conv_conv_b': _L0_conv_in['conv_b'], 'L0_conv_xproj_w': _L0_conv_in['xproj_w'], 'L0_conv_dt_w': _L0_conv_in['dt_w'], 'L0_conv_dt_b': _L0_conv_in['dt_b'], 'L0_conv_A_logs': _L0_conv_in['A_logs'], 'L0_conv_Ds': _L0_conv_in['Ds'], 'L0_conv_out_proj_w': _L0_conv_in['out_proj_w'], 'L1_attn_Wq': _L1_attn_in['Wq'], 'L1_attn_bq': _L1_attn_in['bq'], 'L1_attn_Wk': _L1_attn_in['Wk'], 'L1_attn_bk': _L1_attn_in['bk'], 'L1_attn_Wv': _L1_attn_in['Wv'], 'L1_attn_bv': _L1_attn_in['bv'], 'L1_ffn_router_w': _L1_ffn_in['router_w'], 'L1_ffn_w1': _L1_ffn_in['w1'], 'L1_ffn_w2': _L1_ffn_in['w2'], 'L1_ffn_w3': _L1_ffn_in['w3']}

def reference(x, L0_conv_in_proj_w, L0_conv_conv_w, L0_conv_conv_b, L0_conv_xproj_w, L0_conv_dt_w, L0_conv_dt_b, L0_conv_A_logs, L0_conv_Ds, L0_conv_out_proj_w, L1_attn_Wq, L1_attn_bq, L1_attn_Wk, L1_attn_bk, L1_attn_Wv, L1_attn_bv, L1_ffn_router_w, L1_ffn_w1, L1_ffn_w2, L1_ffn_w3):
    import jax
    import jax.numpy as jnp

    def _L0_conv_ref(x, in_proj_w, conv_w, conv_b, xproj_w, dt_w, dt_b, A_logs, Ds, out_proj_w):
        import jax, jax.numpy as jnp
        import numpy as np
        B, H, W = (2, 16, 16)
        D_MODEL, D_STATE, DT_RANK = (64, 16, 16)
        D_INNER = 2 * D_MODEL

        def _selective_scan(u, delta, A, Bm, Cm, Dv):

            def step(h, inp):
                dt, bt, ct, ut = inp
                h = jnp.exp(dt[..., None] * A) * h + (dt * ut)[..., None] * bt[:, None, :]
                return (h, jnp.einsum('bdn,bn->bd', h, ct))
            h0 = jnp.zeros(u.shape[:2] + (A.shape[1],), u.dtype)
            xs = (jnp.moveaxis(delta, 2, 0), jnp.moveaxis(Bm, 2, 0), jnp.moveaxis(Cm, 2, 0), jnp.moveaxis(u, 2, 0))
            _, ys = jax.lax.scan(step, h0, xs)
            return jnp.moveaxis(ys, 0, 2) + Dv[None, :, None] * u

        def _forward(x, in_proj_w, conv_w, conv_b, xproj_w, dt_w, dt_b, A_logs, Ds, out_proj_w):
            b, h, w, _ = x.shape
            n, r = (D_STATE, DT_RANK)
            l = h * w
            xz = x @ in_proj_w
            xi, z = jnp.split(xz, 2, axis=-1)
            xc = jnp.transpose(xi, (0, 3, 1, 2))
            xc = jax.lax.conv_general_dilated(xc, conv_w, (1, 1), ((1, 1), (1, 1)), dimension_numbers=('NCHW', 'OIHW', 'NCHW'))
            xc = jax.nn.silu(xc + conv_b[None, :, None, None])
            x_dbl = jnp.einsum('bchw,oc->bohw', xc, xproj_w)
            half = x_dbl.shape[1] // 2
            hw_flat = x_dbl[:, :half].reshape(b, half, l)
            wh_flat = jnp.transpose(x_dbl[:, half:], (0, 1, 3, 2)).reshape(b, half, l)

            def split_params(flat):
                dts, bc = (flat[:, :2 * r], flat[:, 2 * r:])
                return ((dts[:, :r], dts[:, r:]), (bc[:, :n], bc[:, n:2 * n]), (bc[:, 2 * n:3 * n], bc[:, 3 * n:]))
            (hd1, hd2), (hb1, hb2), (hc1, hc2) = split_params(hw_flat)
            (wd1, wd2), (wb1, wb2), (wc1, wc2) = split_params(wh_flat)
            hw_x = xc.reshape(b, -1, l)
            wh_x = jnp.transpose(xc, (0, 1, 3, 2)).reshape(b, -1, l)
            xs = jnp.stack([hw_x, hw_x[:, ::-1], wh_x, wh_x[:, ::-1]])
            dt_stack = jnp.stack([hd1, hd2, wd1, wd2])
            Bst = jnp.stack([hb1, hb2, wb1, wb2])
            Cst = jnp.stack([hc1, hc2, wc1, wc2])
            dts = jnp.einsum('kbrl,kdr->kbdl', dt_stack, dt_w)
            delta = jax.nn.softplus(dts + dt_b[:, None, :, None])
            A = -jnp.exp(A_logs)
            ys = jax.vmap(_selective_scan)(xs, delta, A, Bst, Cst, Ds)
            y = ys.sum(0)
            y = jnp.transpose(y, (0, 2, 1)).reshape(b, h, w, -1)
            y = y * jax.nn.silu(z)
            return y @ out_proj_w
        return _forward(x, in_proj_w, conv_w, conv_b, xproj_w, dt_w, dt_b, A_logs, Ds, out_proj_w)

    def _L1_attn_ref(x, Wq, bq, Wk, bk, Wv, bv):
        import jax, jax.numpy as jnp
        import numpy as np
        W = 3
        B, N, D = x.shape
        scale = jnp.asarray(np.sqrt(D), x.dtype)
        Q = x @ Wq.T + bq
        K = x @ Wk.T + bk
        V = x @ Wv.T + bv
        offsets = jnp.arange(-W, W + 1)
        pos = jnp.arange(N)[:, None] + offsets[None, :]
        valid = (pos >= 0) & (pos < N)
        idx = jnp.clip(pos, 0, N - 1)
        Kw = K[:, idx]
        Vw = V[:, idx]
        scores = jnp.einsum('bnd,bnwd->bnw', Q, Kw) / scale
        scores = jnp.where(valid[None], scores, jnp.asarray(-jnp.inf, scores.dtype))
        probs = jax.nn.softmax(scores, axis=-1)
        return jnp.einsum('bnw,bnwd->bnd', probs, Vw)

    def _L1_ffn_ref(x, router_w, w1, w2, w3):
        import jax, jax.numpy as jnp
        import numpy as np
        N_EXPERTS = 8
        TOP_K = 2
        B, T, C = x.shape
        flat = x.reshape(-1, C)
        logits = flat @ router_w.T
        probs = jax.nn.softmax(logits, axis=-1)
        topk_probs, topk_idx = jax.lax.top_k(probs, TOP_K)
        topk_probs = topk_probs / (jnp.sum(topk_probs, axis=-1, keepdims=True) + 1e-09)
        onehot = jax.nn.one_hot(topk_idx, N_EXPERTS, dtype=flat.dtype)
        gates = jnp.einsum('nk,nke->ne', topk_probs, onehot)
        h1 = jnp.einsum('nc,ehc->neh', flat, w1)
        h3 = jnp.einsum('nc,ehc->neh', flat, w3)
        h = jax.nn.silu(h1) * h3
        y = jnp.einsum('neh,ech->nec', h, w2)
        out = jnp.einsum('ne,nec->nc', gates, y)
        return out.reshape(B, T, C)

    def _gn(v, G=32, eps=1e-05):
        B_, H_, W_, C_ = v.shape
        g = v.reshape(B_, H_, W_, G, C_ // G)
        m = jnp.mean(g, axis=(1, 2, 4), keepdims=True)
        s = jnp.var(g, axis=(1, 2, 4), keepdims=True)
        return ((g - m) / jnp.sqrt(s + eps)).reshape(v.shape)

    def _ln_c(v, eps=1e-06):
        m = jnp.mean(v, axis=-1, keepdims=True)
        s = jnp.var(v, axis=-1, keepdims=True)
        return (v - m) / jnp.sqrt(s + eps)

    def _ln_t(v, eps=1e-05):
        m = jnp.mean(v, axis=-1, keepdims=True)
        s = jnp.var(v, axis=-1, keepdims=True)
        return (v - m) / jnp.sqrt(s + eps)

    def _to_tokens(v):
        B_, H_, W_, C_ = v.shape
        return v.reshape(B_, H_ * W_, C_)

    def _from_tokens(t, like):
        return t.reshape(like.shape)
    x = x + _L0_conv_ref(_gn(x), L0_conv_in_proj_w, L0_conv_conv_w, L0_conv_conv_b, L0_conv_xproj_w, L0_conv_dt_w, L0_conv_dt_b, L0_conv_A_logs, L0_conv_Ds, L0_conv_out_proj_w)
    t = _to_tokens(x)
    t = t + _L1_attn_ref(_ln_t(t), L1_attn_Wq, L1_attn_bq, L1_attn_Wk, L1_attn_bk, L1_attn_Wv, L1_attn_bv)
    t = t + _L1_ffn_ref(_ln_t(t), L1_ffn_router_w, L1_ffn_w1, L1_ffn_w2, L1_ffn_w3)
    x = _from_tokens(t, x)
    return x

_drawn_inputs = setup_inputs


def setup_inputs(seed=0):
    import zlib

    import numpy as np

    out = dict(_drawn_inputs(seed))
    spreads = {'L0_conv_conv_b': (0.0, 0.527), 'L0_conv_Ds': (1.0, 0.6)}
    factors = {'L0_conv_in_proj_w': 3.381,
     'L0_conv_conv_w': 3.506,
     'L0_conv_xproj_w': 8.0,
     'L0_conv_dt_w': 8.0,
     'L0_conv_dt_b': 8.0,
     'L0_conv_A_logs': 8.0,
     'L0_conv_out_proj_w': 3.843,
     'L1_attn_bq': 8.114,
     'L1_attn_bk': 64.0,
     'L1_attn_bv': 3.203}
    for name, (base, spread) in spreads.items():
        noise = np.random.default_rng([zlib.crc32(name.encode()), seed]).standard_normal(out[name].shape)
        drawn = base * np.exp(spread * noise) if base else spread * noise
        out[name] = jnp.asarray(drawn.astype(out[name].dtype))
    for name, factor in factors.items():
        out[name] = (out[name] * factor).astype(out[name].dtype)
    return out
```

```python
import concourse.bass as bass
from concourse import mybir
from contextlib import ExitStack

FP32 = mybir.dt.float32
BF16 = mybir.dt.bfloat16
FP32R = mybir.dt.float32r
ALU = mybir.AluOpType
ACT = mybir.ActivationFunctionType
AX = mybir.AxisListType

B, H, W, C = 2, 16, 16, 64
L = H * W
T = B * L
P = 128
NT = T // P
D = 2 * C
N = 16
R = 16
K = 4
G = 32
E = 8
HID = 682
HT = -(-HID // P)
HW = -(-HID // HT)
BODY = 4
PAIRS = E // 2
STEPS = 2 * HT
TAPS = 9
NEG = -1.0e30


def hybrid_kernel(nc, x_grp, x_chan, x_tok, in_proj, conv_w, conv_b, xproj, dt_wb, a_logs, d_skip,
                  out_proj, w_qkv, w_router, w_up, w_down, out):
    ctx = ExitStack()
    with ctx:
        def sb(name, shape, dt=FP32):
            return ctx.enter_context(nc.sbuf_tensor(name, shape, dt))

        def sem(name):
            return ctx.enter_context(nc.semaphore(name))

        ps = ctx.enter_context(nc.psum_tensor("ps", [P, 8, 512], FP32))

        xg = sb("xg", [B * G, 2 * L])
        xc = sb("xc", [C, T])
        xt = sb("xt", [P, NT, C])
        w_in = sb("w_in", [C, 2 * D])
        w_conv = sb("w_conv", [D, TAPS, D])
        b_conv = sb("b_conv", [D, 1])
        w_xp = sb("w_xp", [D, K // 2, 2 * R + 4 * N])
        w_rep = sb("w_rep", [D, K, 3 * 2 * N + R])
        w_dt = sb("w_dt", [P, K, D])
        a_log = sb("a_log", [D, K * N])
        a_exp = sb("a_exp", [D, K * N])
        a_neg = sb("a_neg", [D, K * N])
        dsk = sb("dsk", [D, K])
        w_out = sb("w_out", [D, C])
        wqkv = sb("wqkv", [C + 1, 3, C])
        w_rt = sb("w_rt", [C, E])
        wraw = sb("wraw", [2 * C, 2, 2, 2, HID])
        wup = sb("wup", [2 * C, 2, 2, 2, HID], FP32R)
        wdn = sb("wdn", [P, 2, 2, HT, C])

        ident = sb("ident", [P, P])
        flip = sb("flip", [D, D])
        sel_row = sb("sel_row", [3 * 2 * N, 2 * N], BF16)
        sel_grp = sb("sel_grp", [B * G, B, G, 2])
        band = sb("band", [P, 2, L])
        rank = sb("rank", [P, E])

        st_g = sb("st_g", [B * G, 6])
        mr_g = sb("mr_g", [B * G, 2])
        sd_g = sb("sd_g", [B * G, 1])
        mr_c = sb("mr_c", [C, B, 2])
        xn = sb("xn", [C, T])
        xpad = sb("xpad", [D, B, H + 2, W + 2])
        zs = sb("zs", [D, T])
        u = sb("u", [D, K, T])
        d_diag = sb("d_diag", [D, K, D])
        pf = sb("pf", [P, K, T])
        bc = sb("bc", [3 * 2 * N, K, T], BF16)
        r1 = sb("r1", [3 * 2 * N, T])
        ab = sb("ab", [D, T])
        ex = sb("ex", [D, T])
        lg = sb("lg", [D, T])
        cr = sb("cr", [D, T])
        sm = sb("sm", [D, T])
        delta = sb("delta", [D, 2, T])
        du = sb("du", [D, 2, T])
        rings = sb("rings", [D, 4, BODY * T])
        da = rings[:, 0].rearrange("p (q b l) -> p q b l", q=BODY, b=B)
        hs, cs, hc = (rings[:, r].rearrange("p (q t) -> p q t", q=BODY) for r in (1, 2, 3))
        wnext = rings[:].rearrange("p r n -> p (r n)")[:, 0:2 * 4 * HID].bitcast(FP32R).rearrange(
            "p (s a b h) -> p s a b h", s=2, a=2, b=2)
        yg = sb("yg", [D, T])

        t1 = sb("t1", [P, NT, C])
        t2 = sb("t2", [P, NT, C])
        st = sb("st", [P, NT, 6])
        mv = sb("mv", [P, NT, 2])
        ve = sb("ve", [P, NT])
        sd = sb("sd", [P, NT])
        rs = sb("rs", [P, NT])
        dm = sb("dm", [P, NT, C])
        tn = sb("tn", [P, NT, C])
        tn2 = sb("tn2", [P, NT, 2, C])
        tnT = sb("tnT", [C + 1, T])
        qT = sb("qT", [C, T])
        kT = sb("kT", [C, T])
        v = sb("v", [P, NT, C])
        sc = sb("sc", [P, NT, L])
        mx = sb("mx", [P, NT])
        nm = sb("nm", [P, NT])
        pr = sb("pr", [P, NT, L])
        sums = sb("sums", [P, NT])
        rsum = sb("rsum", [P, NT])
        prT = sb("prT", [P, NT, 2, P])
        ov = sb("ov", [P, NT, C])
        fT = sb("fT", [C, T])
        fh = sb("fh", [P, T], FP32R)
        fl = sb("fl", [P, T], FP32R)

        lo = sb("lo", [P, NT, E])
        le = sb("le", [P, NT, E])
        pb = sb("pb", [P, NT, E])
        g1 = sb("g1", [P, NT])
        g2 = sb("g2", [P, NT])
        g3 = sb("g3", [P, NT])
        m1 = sb("m1", [P, NT])
        m2 = sb("m2", [P, NT])
        key = sb("key", [P, NT, E])
        oh1 = sb("oh1", [P, NT, E])
        oh2 = sb("oh2", [P, NT, E])
        pb2 = sb("pb2", [P, NT, E])
        gate = sb("gate", [P, NT, E])
        si = sb("si", [P, 2, T])
        gl = sb("gl", [P, 4, T])
        ysb = sb("ysb", [P, T])
        gy = sb("gy", [P, NT, 2, C])
        acc = sb("acc", [P, NT, 2, C])
        res = sb("res", [P, NT, C])
        warm = sb("warm", [1, 1])

        x_in, xt_in, win_in, conv_in, prm_in, qkv_in, out_in = (
            sem(n) for n in ("x_in", "xt_in", "win_in", "conv_in", "prm_in", "qkv_in", "out_in"))
        raw_in = [sem(f"raw_in{i}") for i in range(2)]
        down_in = [sem(f"down_in{i}") for i in range(2)]
        slot_ready = [sem(f"slot_ready{i}") for i in range(2)]
        w_rounded, w_split, fT_kept = (sem(n) for n in ("w_rounded", "w_split", "fT_kept"))
        stored = sem("stored")
        pool_step = sem("pool_step")
        dve_step = sem("dve_step")
        warm_set = sem("warm_set")
        act_step = sem("act_step")
        pad_zero = sem("pad_zero")
        ones_set = sem("ones_set")
        da_zero = sem("da_zero")
        sd_ready, mr_ready, mrc_ready, mrc_copied, xn_ready = (
            sem(n) for n in ("sd_ready", "mr_ready", "mrc_ready", "mrc_copied", "xn_ready"))
        flip_ready = sem("flip_ready")
        xi_ready, xi_padded, conv_ready, u_ready, z_done, proj_ready, proj_kept, hi_ready = (
            sem(n) for n in ("xi_ready", "xi_padded", "conv_ready", "u_ready", "z_done", "proj_ready",
                             "proj_kept", "hi_ready"))
        aexp_ready, aneg_ready, diag_ready = (sem(n) for n in ("aexp_ready", "aneg_ready", "diag_ready"))
        dt_ready, log_ready, bc_ready, delta_ready, du_ready = (
            sem(n) for n in ("dt_ready", "log_ready", "bc_ready", "delta_ready", "du_ready"))
        b_ready, b_used, c_ready, c_kept, da_ready, scanned, weighted, summed = (
            sem(n) for n in ("b_ready", "b_used", "c_ready", "c_kept", "da_ready", "scanned",
                             "weighted", "summed"))
        y_ready, yg_ready, op_ready = (sem(n) for n in ("y_ready", "yg_ready", "op_ready"))
        ve_ready, sdt_ready, tn_ready, tnT_ready, tnT_kept = (
            sem(n) for n in ("ve_ready", "sdt_ready", "tn_ready", "tnT_ready", "tnT_kept"))
        qk_ready, v_ready, q_kept, k_kept, v_kept, s_ready, mx_ready, pr_ready = (
            sem(n) for n in ("qk_ready", "v_ready", "q_kept", "k_kept", "v_kept", "s_ready",
                             "mx_ready", "pr_ready"))
        prT_ready, prT_kept_a, prT_kept_d, o_ready = (
            sem(n) for n in ("prT_ready", "prT_kept_a", "prT_kept_d", "o_ready"))
        fT_ready, lo_ready, lsub_ready, le_ready = (
            sem(n) for n in ("fT_ready", "lo_ready", "lsub_ready", "le_ready"))
        up_ready, silu_ready, glu_ready, down_done, y_kept, yT_ready, y_added, res_ready = (
            sem(n) for n in ("up_ready", "silu_ready", "glu_ready", "down_done", "y_kept", "yT_ready",
                             "y_added", "res_ready"))

        block = ctx.enter_context(nc.Block())

        def wait(eng, s, value):
            if isinstance(value, int) and value <= 0:
                return
            eng.wait_ge(s, value)

        def states_loop(eng, body):
            for k in range(K):
                if k == 0:
                    body(0, 0)
                yield k
                with eng.Fori(1 if k == 0 else 0, N // BODY) as i:
                    body(k, i)

        BANK_B, BANK_X, BANK_C, BANK_Y, BANK_DT = 0, 2, 4, 6, 7
        PROJ_BANKS = (0, 1, 3, 5)
        BANK_H, BANK_O = 0, 6

        @block.sync
        def _(sp):
            sp.dma_start(xg[:], x_grp).then_inc(x_in, 16)
            sp.dma_start(xc[:], x_chan).then_inc(x_in, 16)
            sp.dma_start(w_in[:], in_proj).then_inc(win_in, 16)
            sp.dma_start(w_conv[:], conv_w).then_inc(conv_in, 16)
            sp.dma_start(xt[:], x_tok).then_inc(xt_in, 16)
            sp.dma_start(w_out[:], out_proj).then_inc(out_in, 16)
            sp.dma_start(wqkv[:], w_qkv).then_inc(qkv_in, 16)
            sp.dma_start(w_rt[:], w_router).then_inc(qkv_in, 16)
            def load_raw(pair):
                for half in range(2):
                    sp.dma_start(wraw[half * C:(half + 1) * C, pair % 2],
                                 w_up[:, 2 * pair:2 * pair + 2]).then_inc(raw_in[pair % 2], 16)

            def load_down(pair):
                for e in range(2):
                    sp.dma_start(wdn[0:HW, pair % 2, e, 0:HT - 1, :],
                                 w_down[2 * pair + e, 0:(HT - 1) * HW, :].rearrange("(j p) c -> p j c", p=HW)
                                 ).then_inc(down_in[pair % 2], 16)
                    sp.dma_start(wdn[0:HID - (HT - 1) * HW, pair % 2, e, HT - 1, :],
                                 w_down[2 * pair + e, (HT - 1) * HW:HID, :]).then_inc(down_in[pair % 2], 16)

            for pair in range(2):
                load_raw(pair)
                load_down(pair)
            for pair in range(2, PAIRS):
                sp.wait_ge(slot_ready[pair % 2], 1)
                load_raw(pair)
            for pair in range(2, PAIRS):
                sp.wait_ge(w_split, pair - 1)
                sp.wait_ge(up_ready, STEPS * (pair - 1))
                sp.dma_start(wup[:, pair % 2].rearrange("p a b h -> p (a b h)").bitcast(FP32),
                             wnext[:, pair % 2].rearrange("p a b h -> p (a b h)").bitcast(FP32)).then_inc(slot_ready[pair % 2], 16)
                sp.wait_ge(down_done, 2 + HT * (pair - 1))
                load_down(pair)
            sp.wait_ge(res_ready, 1)
            sp.dma_start(out, res[:]).then_inc(stored, 16)
            sp.wait_ge(stored, 16)

        @block.gpsimd
        def _(pool):
            done = [0]

            def step(ins):
                done[0] += 1
                ins.then_inc(pool_step, 1)

            def wait_steps():
                pool.wait_ge(pool_step, done[0])

            step(nc.gpsimd.memset(sel_grp[:], 0.0))
            step(nc.gpsimd.memset(ident[:], 0.0))
            step(nc.gpsimd.memset(sel_row[:], 0.0))
            step(nc.gpsimd.memset(flip[:], 0.0))
            wait_steps()
            step(nc.gpsimd.affine_select(out=sel_grp[:], in_=sel_grp[:], compare_op=ALU.not_equal, fill=1.0,
                                         base=0, pattern=[[-G, B], [-1, G], [0, 2]], channel_multiplier=1))
            step(nc.gpsimd.affine_select(out=ident[:], in_=ident[:], compare_op=ALU.not_equal, fill=1.0,
                                         base=0, pattern=[[-1, P]], channel_multiplier=1))
            step(nc.gpsimd.affine_select(out=flip[:], in_=flip[:], compare_op=ALU.not_equal, fill=1.0,
                                         base=1 - D, pattern=[[1, D]], channel_multiplier=1))
            for part in range(3):
                wait_steps()
                step(nc.gpsimd.affine_select(out=sel_row[:], in_=sel_row[:], compare_op=ALU.not_equal, fill=1.0,
                                             base=-2 * N * part, pattern=[[-1, 2 * N]], channel_multiplier=1))
            pool.wait_ge(prm_in, 16 * 6)
            for k in range(K):
                half, odd = k // 2, k % 2
                for col, row in [(0, 2 * R + N * odd), (N, 2 * R + 2 * N + N * odd), (6 * N, R * odd)]:
                    for copy in range(3 if col < 6 * N else 1):
                        at = col + 2 * N * copy
                        step(nc.gpsimd.tensor_copy(w_rep[:, k, at:at + N], w_xp[:, half, row:row + N]))
            step(nc.gpsimd.memset(band[:], 0.0))
            step(nc.gpsimd.iota(rank[:], pattern=[[-1, E]], base=E, channel_multiplier=0,
                                allow_small_or_imprecise_dtypes=True))
            for sign in (1, -1):
                wait_steps()
                step(nc.gpsimd.affine_select(out=band[:], in_=band[:], compare_op=ALU.is_ge, fill=NEG, base=3,
                                             pattern=[[-sign * P, 2], [sign, L]], channel_multiplier=-sign))

            def body(k, i):
                for half in range(2):
                    n = k * N + BODY * i + 2 * half
                    two = slice(2 * half, 2 * half + 2)
                    wait(pool, scanned, n + 2)
                    wait(pool, c_kept, k * N // 2 + BODY // 2 * i + half + 1)
                    wait(pool, summed, k * N // 2 + BODY // 2 * i + half - 1)
                    nc.gpsimd.tensor_tensor(hc[:, two], hs[:, two], cs[:, two], ALU.mult).then_inc(weighted, 1)

            for _ in states_loop(nc.gpsimd, body):
                pass

            pool.wait_ge(weighted, K * N // 2)
            for pair in range(PAIRS):
                to = wup if pair < 2 else wnext
                pool.wait_ge(raw_in[pair % 2], 32 * (pair // 2 + 1))
                if pair == 2:
                    pool.wait_ge(summed, K * N // 2)
                if pair >= 2:
                    nc.gpsimd.tensor_copy(to[:, pair % 2], wraw[:, pair % 2]).then_inc(w_rounded, 1)
                pool.wait_ge(w_rounded, pair + 1)
                nc.gpsimd.tensor_tensor(to[C:2 * C, pair % 2], wraw[C:2 * C, pair % 2],
                                        to[C:2 * C, pair % 2].bitcast(FP32), ALU.subtract
                                        ).then_inc(slot_ready[pair] if pair < 2 else w_split, 1)
                if pair < 2:
                    pool.wait_ge(slot_ready[pair], 1)
                else:
                    pool.wait_ge(w_split, pair - 1)

        @block.scalar
        def _(act):
            act.dma_start(b_conv[:], conv_b).then_inc(prm_in, 16)
            act.dma_start(w_xp[:], xproj).then_inc(prm_in, 16)
            act.dma_start(a_log[:], a_logs).then_inc(prm_in, 16)
            act.dma_start(dsk[:], d_skip).then_inc(prm_in, 16)
            act.dma_start(w_dt[3 * 2 * N:3 * 2 * N + R + 1], dt_wb).then_inc(prm_in, 16)
            act.wait_ge(warm_set, 1)
            act.dma_start(warm[:], conv_b[0:1]).then_inc(prm_in, 16)
            act.wait_ge(dve_step, 3)
            nc.scalar.activation(sd_g[:], mr_g[:, 1:2], ACT.Sqrt).then_inc(sd_ready, 1)
            act.wait_ge(xi_ready, 1)
            act.wait_ge(pad_zero, 1)
            for b in range(B):
                last = nc.scalar.activation(xpad[:, b, 1:H + 1, 1:W + 1],
                                            ps[:, 0, b * L:(b + 1) * L].rearrange("p (h w) -> p h w", h=H), ACT.Copy)
                last.then_inc(xi_padded, 1)
            act.wait_ge(xi_ready, 2)
            nc.scalar.activation(zs[:], ps[:, 1, :], ACT.Silu).then_inc(z_done, 1)
            act.wait_ge(prm_in, 16 * 6)
            act.wait_ge(conv_ready, 1)
            nc.scalar.activation(u[:, 0, :], ps[:, 2, :], ACT.Silu, bias=b_conv[:]).then_inc(u_ready, 1)
            for k, bank in ((2, 2), (1, 4), (3, 4)):
                if k == 1:
                    act.wait_ge(flip_ready, 1)
                src, dst = ps[:, bank, :], u[:, k, :]
                if k // 2:
                    src = src.rearrange("p (b h w) -> p b w h", b=B, h=H)
                    dst = dst.rearrange("p (b w h) -> p b w h", b=B, w=W)
                if k == 2:
                    nc.scalar.activation(dst, src, ACT.Silu, bias=b_conv[:]).then_inc(u_ready, 1)
                else:
                    nc.scalar.activation(dst, src, ACT.Copy).then_inc(u_ready, 1)
            nc.scalar.activation(a_exp[:], a_log[:], ACT.Exp).then_inc(aexp_ready, 1)
            for k in range(K):
                act.wait_ge(proj_ready, k + 1)
                if k == 0:
                    act.wait_ge(ones_set, 1)
                nc.scalar.activation(pf[0:6 * N + R, k, :], ps[0:6 * N + R, PROJ_BANKS[k], :],
                                     ACT.Copy).then_inc(proj_kept, 1)
                act.wait_ge(proj_kept, k + 1)
                nc.scalar.activation(bc[:, k, :], pf[0:6 * N, k, :], ACT.Copy).then_inc(hi_ready, 1)

            def softplus_parts(k):
                act.wait_ge(dt_ready, k + 1)
                nc.scalar.activation(ab[:], ps[:, BANK_DT, :], ACT.Abs).then_inc(act_step, 1)
                act.wait_ge(act_step, 2 * k + 1)
                nc.scalar.activation(ex[:], ab[:], ACT.Exp, scale=-1.0).then_inc(act_step, 1)
                act.wait_ge(act_step, 2 * k + 2)
                nc.scalar.activation(lg[:], ex[:], ACT.Ln, bias=1.0).then_inc(log_ready, 1)

            softplus_parts(0)

            def body(k, i):
                for q in range(BODY):
                    n = k * N + BODY * i + q
                    wait(act, scanned, n - BODY + 1)
                    col = BODY * i + q
                    nc.scalar.activation(da[:, q, :, 1:L],
                                         delta[:, k % 2, :].rearrange("p (b l) -> p b l", b=B)[:, :, 1:L], ACT.Exp,
                                         scale=a_neg[:, bass.ds(k * N + col, 1)]).then_inc(da_ready, 1)
                    if q % 2:
                        g = k * N // 2 + BODY // 2 * i + q // 2
                        two = slice(q - 1, q + 1)
                        act.wait_ge(c_ready, g + 1)
                        wait(act, weighted, g - 1)
                        nc.scalar.activation(cs[:, two], ps[:, BANK_C:BANK_C + 2, :], ACT.Copy).then_inc(c_kept, 1)

            act.wait_ge(aneg_ready, 1)
            act.wait_ge(delta_ready, 1)
            act.wait_ge(da_zero, 1)
            for k in states_loop(nc.scalar, body):
                if k + 1 < K:
                    softplus_parts(k + 1)
                if k:
                    act.wait_ge(delta_ready, k + 1)

            act.wait_ge(ve_ready, 1)
            nc.scalar.activation(sd[:], ve[:], ACT.Sqrt).then_inc(sdt_ready, 1)
            act.wait_ge(qk_ready, 1)
            nc.scalar.activation(qT[:], ps[0:C, 2, :], ACT.Copy).then_inc(q_kept, 1)
            act.wait_ge(v_ready, 1)
            nc.scalar.activation(v[:], ps[:, 4, 0:NT * C].rearrange("p (t c) -> p t c", t=NT), ACT.Copy).then_inc(v_kept, 1)
            act.wait_ge(mx_ready, 1)
            for t in range(NT):
                nc.scalar.activation(pr[:, t, :], sc[:, t, :], ACT.Exp, bias=nm[:, t:t + 1], scale=C ** -0.5,
                                     accum_out=sums[:, t:t + 1]).then_inc(pr_ready, 1)
            act.wait_ge(prT_ready, 1)
            nc.scalar.activation(prT[:, 0:2], ps[:, 0, :], ACT.Copy).then_inc(prT_kept_a, 1)
            act.wait_ge(ve_ready, 2)
            nc.scalar.activation(sd[:], ve[:], ACT.Sqrt).then_inc(sdt_ready, 1)
            act.wait_ge(fT_ready, 1)
            act.wait_ge(glu_ready, 3)
            nc.scalar.activation(fT[:], ps[0:C, 2, :], ACT.Copy).then_inc(fT_kept, 1)
            act.wait_ge(lsub_ready, 1)
            nc.scalar.activation(le[:], lo[:], ACT.Exp).then_inc(le_ready, 1)

            with nc.scalar.Fori(0, PAIRS // 2) as it:
                for half in range(2):
                    for s in range(STEPS):
                        S = 2 * STEPS * it + STEPS * half + s
                        rows = HW if s // 2 < HT - 1 else HID - (HT - 1) * HW
                        act.wait_ge(up_ready, S + 1)
                        act.wait_ge(glu_ready, S + 2)
                        nc.scalar.activation(si[0:rows, s % 2, :], ps[0:rows, BANK_H + 2 * (s % 3), :],
                                             ACT.Silu).then_inc(silu_ready, 1)
                        if half == 1 and s == 3:
                            act.wait_ge(down_done, 2 + HT * (2 * it + 1))
                            nc.scalar.activation(ysb[:], ps[:, BANK_O, :], ACT.Copy).then_inc(y_kept, 1)
                act.wait_ge(down_done, 2 + HT * (2 * it + 2))
                act.wait_ge(yT_ready, 2 * it + 1)
                nc.scalar.activation(ysb[:], ps[:, BANK_O + 1, :], ACT.Copy).then_inc(y_kept, 1)

        @block.vector
        def _(dve):
            done = [0]

            def chain(ins):
                done[0] += 1
                ins.then_inc(dve_step, 1)
                dve.wait_ge(dve_step, done[0])

            dve.wait_ge(x_in, 32)
            chain(nc.vector.bn_stats(st_g[:], xg[:]))
            chain(nc.vector.bn_aggr(mr_g[:], st_g[:]))
            chain(nc.vector.tensor_scalar(mr_g[:, 1:2], mr_g[:, 1:2], 1e-5, None, ALU.add))
            nc.vector.memset(warm[:], 0.0).then_inc(warm_set, 1)
            nc.vector.memset(xpad[:], 0.0).then_inc(pad_zero, 1)
            nc.vector.memset(pf[6 * N:P], 1.0).then_inc(ones_set, 1)
            nc.vector.memset(da[:, :, :, 0:1], 0.0).then_inc(da_zero, 1)
            dve.wait_ge(sd_ready, 1)
            nc.vector.reciprocal(mr_g[:, 1:2], sd_g[:]).then_inc(mr_ready, 1)
            dve.wait_ge(mrc_ready, 1)
            nc.vector.tensor_copy(mr_c[:], ps[0:C, 7, 0:2 * B].rearrange("p (b s) -> p b s", b=B)).then_inc(mrc_copied, 1)
            dve.wait_ge(mrc_copied, 1)
            for b in range(B):
                last = nc.vector.tensor_scalar(xn[:, b * L:(b + 1) * L], xc[:, b * L:(b + 1) * L], mr_c[:, b, 0:1],
                                               mr_c[:, b, 1:2], ALU.subtract, ALU.mult)
                last.then_inc(xn_ready, 1)
            dve.wait_ge(prm_in, 16 * 6)
            dve.wait_ge(pool_step, 6)
            for k in range(K):
                nc.vector.tensor_scalar(d_diag[:, k, :], ident[:], dsk[:, k:k + 1], None,
                                        ALU.mult).then_inc(diag_ready, 1)
            dve.wait_ge(aexp_ready, 1)
            nc.vector.tensor_scalar(a_neg[:], a_exp[:], -1.0, None, ALU.mult).then_inc(aneg_ready, 1)

            def split_and_softplus(k):
                dve.wait_ge(hi_ready, k + 1)
                chain(nc.vector.tensor_tensor(r1[:], pf[0:6 * N, k, :], bc[:, k, :], ALU.subtract))
                nc.vector.tensor_copy(bc[2 * N:4 * N, k, :], r1[2 * N:4 * N, :]).then_inc(bc_ready, 1)
                chain(nc.vector.tensor_copy(bc[4 * N:6 * N, k, :], r1[4 * N:6 * N, :]))
                nc.vector.tensor_tensor(bc[4 * N:6 * N, k, :], r1[4 * N:6 * N, :], bc[4 * N:6 * N, k, :],
                                        ALU.subtract).then_inc(bc_ready, 1)
                dve.wait_ge(log_ready, k + 1)
                chain(nc.vector.tensor_scalar(cr[:], ex[:], 1.0, -1.0, ALU.add, ALU.add))
                chain(nc.vector.tensor_tensor(sm[:], ex[:], cr[:], ALU.subtract))
                chain(nc.vector.tensor_tensor(cr[:], sm[:], lg[:], ALU.add))
                nc.vector.scalar_tensor_tensor(delta[:, k % 2, :], ps[:, BANK_DT, :], 0.0, cr[:], ALU.max,
                                               ALU.add).then_inc(delta_ready, 1)
                dve.wait_ge(delta_ready, k + 1)
                dve.wait_ge(u_ready, K)
                nc.vector.tensor_tensor(du[:, k % 2, :], delta[:, k % 2, :], u[:, k, :], ALU.mult).then_inc(du_ready, 1)
                dve.wait_ge(du_ready, k + 1)

            def body(k, i):
                def times_b(q):
                    n = k * N + BODY * i + q
                    dve.wait_ge(b_ready, n + 1)
                    wait(dve, scanned, n - 1)
                    nc.vector.tensor_tensor(ps[:, BANK_X + q % 2, :], ps[:, BANK_B + q % 2, :], du[:, k % 2, :],
                                            ALU.mult).then_inc(b_used, 1)

                def scan(q):
                    n = k * N + BODY * i + q
                    dve.wait_ge(da_ready, n + 1)
                    dve.wait_ge(b_used, n + 1)
                    wait(dve, weighted, k * N // 2 + BODY // 2 * i + q // 2 - 1)
                    nc.vector.tensor_tensor_scan(hs[:, q, :], da[:, q].rearrange("p b l -> p (b l)"),
                                                 ps[:, BANK_X + q % 2, :], 0.0, ALU.mult, ALU.add).then_inc(scanned, 1)

                times_b(0)
                for q in range(1, BODY):
                    times_b(q)
                    scan(q - 1)
                scan(BODY - 1)

            split_and_softplus(0)
            for k in states_loop(nc.vector, body):
                if k:
                    pass
                if k + 1 < K and k == 0:
                    split_and_softplus(1)
                elif k + 1 < K:
                    split_and_softplus(k + 1)
                if k == 1:
                    for pair in range(2):
                        dve.wait_ge(raw_in[pair], 32)
                        nc.vector.tensor_copy(wup[:, pair], wraw[:, pair]).then_inc(w_rounded, 1)

            dve.wait_ge(y_ready, 1)
            dve.wait_ge(z_done, 1)
            nc.vector.tensor_tensor(yg[:], ps[:, BANK_Y, :], zs[:], ALU.mult).then_inc(yg_ready, 1)
            dve.wait_ge(op_ready, 1)
            dve.wait_ge(xt_in, 16)

            def over(ap, n):
                return ap.unsqueeze(2).broadcast_to([P, NT, n])

            def layer_norm(src, turn):
                for t in range(NT):
                    chain(nc.vector.bn_stats(st[:, t, :], src[:, t, :]))
                for t in range(NT):
                    chain(nc.vector.bn_aggr(mv[:, t, :], st[:, t, :]))
                chain(nc.vector.tensor_scalar(ve[:], mv[:, :, 1], 1e-5, None, ALU.add))
                nc.vector.tensor_tensor(dm[:], src[:], over(mv[:, :, 0], C), ALU.subtract).then_inc(ve_ready, 1)
                dve.wait_ge(ve_ready, turn)
                dve.wait_ge(sdt_ready, turn)
                chain(nc.vector.reciprocal(rs[:], sd[:]))
                if turn == 1:
                    normed = nc.vector.tensor_tensor(tn[:], dm[:], over(rs[:], C), ALU.mult)
                else:
                    normed = nc.vector.tensor_tensor(tn2[:], dm[:].unsqueeze(2).broadcast_to([P, NT, 2, C]),
                                                     rs[:].unsqueeze(2).unsqueeze(3).broadcast_to([P, NT, 2, C]), ALU.mult)
                normed.then_inc(tn_ready, 1)

            chain(nc.vector.tensor_tensor(t1[:], xt[:], ps[:, 0, 0:NT * C].rearrange("p (t c) -> p t c", t=NT), ALU.add))
            layer_norm(t1, 1)
            nc.vector.memset(tnT[C:C + 1, :], 1.0).then_inc(tnT_kept, 1)
            dve.wait_ge(tnT_ready, 1)
            nc.vector.tensor_copy(tnT[0:C, :], ps[0:C, 1, :]).then_inc(tnT_kept, 1)
            dve.wait_ge(qk_ready, 2)
            nc.vector.tensor_copy(kT[:], ps[0:C, 3, :]).then_inc(k_kept, 1)
            for b in range(B):
                dve.wait_ge(s_ready, b + 1)
                chain(nc.vector.tensor_tensor(sc[:, 2 * b:2 * b + 2, :],
                                              ps[:, 5 + b, :].rearrange("p (t l) -> p t l", t=2), band[:], ALU.add))
            chain(nc.vector.tensor_reduce(mx[:], sc[:], AX.X, ALU.max))
            nc.vector.tensor_scalar(nm[:], mx[:], -(C ** -0.5), None, ALU.mult).then_inc(mx_ready, 1)
            dve.wait_ge(prT_ready, 2)
            nc.vector.tensor_copy(prT[:, 2:4], ps[:, 1, :].rearrange("p (t k q) -> p t k q", t=2, k=2)).then_inc(prT_kept_d, 1)
            dve.wait_ge(pr_ready, NT)
            chain(nc.vector.reciprocal(rsum[:], sums[:]))
            dve.wait_ge(o_ready, 1)
            chain(nc.vector.tensor_tensor(ov[:], ps[:, 7, 0:NT * C].rearrange("p (t c) -> p t c", t=NT), over(rsum[:], C), ALU.mult))
            chain(nc.vector.tensor_tensor(t2[:], t1[:], ov[:], ALU.add))
            layer_norm(t2, 2)
            nc.vector.tensor_copy(acc[:, :, 0, :], t2[:]).then_inc(glu_ready, 1)
            nc.vector.memset(acc[:, :, 1, :], 0.0).then_inc(y_added, 1)
            dve.wait_ge(fT_ready, 1)
            nc.vector.tensor_copy(fh[:], ps[:, 2, :]).then_inc(glu_ready, 1)
            dve.wait_ge(glu_ready, 2)
            nc.vector.tensor_tensor(fl[:], ps[:, 2, :], fh[:].bitcast(FP32), ALU.subtract).then_inc(glu_ready, 1)

            dve.wait_ge(lo_ready, 2)
            lps = ps[:, 7, 0:NT * E].rearrange("p (t e) -> p t e", t=NT)
            chain(nc.vector.tensor_reduce(g1[:], lps, AX.X, ALU.max))
            nc.vector.tensor_tensor(lo[:], lps, over(g1[:], E), ALU.subtract).then_inc(lsub_ready, 1)
            dve.wait_ge(le_ready, 1)
            chain(nc.vector.tensor_reduce(g2[:], le[:], AX.X, ALU.add))
            chain(nc.vector.reciprocal(g3[:], g2[:]))
            chain(nc.vector.tensor_tensor(pb[:], le[:], over(g3[:], E), ALU.mult))
            ranks = rank[:].unsqueeze(1).broadcast_to([P, NT, E])

            def pick_largest(src, top, one_hot):
                chain(nc.vector.tensor_reduce(top[:], src[:], AX.X, ALU.max))
                chain(nc.vector.tensor_tensor(key[:], src[:], over(top[:], E), ALU.is_equal))
                chain(nc.vector.tensor_tensor(key[:], key[:], ranks, ALU.mult))
                chain(nc.vector.tensor_reduce(g1[:], key[:], AX.X, ALU.max))
                chain(nc.vector.tensor_tensor(one_hot[:], key[:], over(g1[:], E), ALU.is_equal))

            pick_largest(pb, m1, oh1)
            chain(nc.vector.scalar_tensor_tensor(pb2[:], oh1[:], -4.0, pb[:], ALU.mult, ALU.add))
            pick_largest(pb2, m2, oh2)
            chain(nc.vector.tensor_tensor(g2[:], m1[:], m2[:], ALU.add))
            chain(nc.vector.tensor_scalar(g2[:], g2[:], 1e-9, None, ALU.add))
            chain(nc.vector.reciprocal(g3[:], g2[:]))
            chain(nc.vector.tensor_tensor(oh1[:], oh1[:], oh2[:], ALU.add))
            chain(nc.vector.tensor_tensor(pb[:], pb[:], over(g3[:], E), ALU.mult))
            chain(nc.vector.tensor_tensor(gate[:], oh1[:], pb[:], ALU.mult))

            with nc.vector.Fori(0, PAIRS // 2) as it:
                def add_pair(half):
                    pair = 2 * it + half
                    dve.wait_ge(yT_ready, pair + 1)
                    g_ap = gate[:, :, bass.ds(2 * pair, 2)].unsqueeze(3).broadcast_to([P, NT, 2, C])
                    nc.vector.tensor_tensor(gy[:], ps[:, BANK_O + half, :].rearrange("p (t e c) -> p t e c", t=NT, e=2),
                                            g_ap, ALU.mult).then_inc(y_added, 1)
                    dve.wait_ge(y_added, 2 * pair + 2)
                    nc.vector.tensor_tensor(acc[:], acc[:], gy[:], ALU.add).then_inc(y_added, 1)
                    dve.wait_ge(y_added, 2 * pair + 3)

                for half in range(2):
                    for s in range(STEPS):
                        S = 2 * STEPS * it + STEPS * half + s
                        rows = HW if s // 2 < HT - 1 else HID - (HT - 1) * HW
                        dve.wait_ge(silu_ready, S + 1)
                        dve.wait_ge(down_done, STEPS * it + (STEPS * half + s) // 2 + 1)
                        nc.vector.tensor_tensor(gl[0:rows, s % 4, :], ps[0:rows, BANK_H + 2 * (s % 3) + 1, :],
                                                si[0:rows, s % 2, :], ALU.mult).then_inc(glu_ready, 1)
                        if half == 1 and s == 5:
                            add_pair(0)
                add_pair(1)
            nc.vector.tensor_tensor(res[:], acc[:, :, 0, :], acc[:, :, 1, :], ALU.add).then_inc(res_ready, 1)

        @block.tensor
        def _(pe):
            pe.wait_ge(mr_ready, 1)
            pe.wait_ge(pool_step, 5)
            for b in range(B):
                last = nc.tensor.matmul(ps[0:C, 7, 2 * b:2 * b + 2], sel_grp[:, b].rearrange("p g c -> p (g c)"),
                                        mr_g[:], start=True, stop=True)
            last.then_inc(mrc_ready, 1)
            pe.wait_ge(xn_ready, B)
            pe.wait_ge(win_in, 16)
            for half in range(2):
                nc.tensor.matmul(ps[:, half, :], w_in[:, half * D:(half + 1) * D], xn[:], start=True,
                                 stop=True).then_inc(xi_ready, 1)
            pe.wait_ge(xi_padded, B)
            pe.wait_ge(conv_in, 16)
            for tap in range(TAPS):
                last = nc.tensor.matmul(ps[:, 2, :], w_conv[:, tap, :],
                                        xpad[:, :, tap // 3:tap // 3 + H, tap % 3:tap % 3 + W],
                                        start=(tap == 0), stop=(tap == TAPS - 1))
            last.then_inc(conv_ready, 1)
            pe.wait_ge(pool_step, 10 + 7 * K)
            pe.wait_ge(u_ready, 1)
            nc.tensor.matmul(ps[:, 4, :], flip[:], u[:, 0, :], start=True, stop=True).then_inc(flip_ready, 1)
            pe.wait_ge(z_done, 1)
            for k in range(K):
                pe.wait_ge(u_ready, 1 if k < 2 else 2)
                nc.tensor.matmul(ps[0:6 * N + R, PROJ_BANKS[k], :], w_rep[:, k, :],
                                 u[:, 2 * (k // 2), :], start=True, stop=True).then_inc(proj_ready, 1)

            def dt_product(k):
                pe.wait_ge(proj_kept, k + 1)
                if k == 0:
                    pe.wait_ge(ones_set, 1)
                    pe.wait_ge(mrc_copied, 1)
                    pe.wait_ge(prm_in, 16 * 6)
                else:
                    pe.wait_ge(delta_ready, k)
                nc.tensor.matmul(ps[:, BANK_DT, :], w_dt[6 * N:6 * N + R + 1, k, :], pf[6 * N:6 * N + R + 1, k, :],
                                 start=True, stop=True).then_inc(dt_ready, 1)

            def skip(k):
                nc.tensor.matmul(ps[:, BANK_Y, :], d_diag[:, k, :], u[:, k, :], start=(k == 0), stop=(k == K - 1))

            def sum_states(half, g):
                wait(pe, weighted, g + 1)
                for q in range(2):
                    last = nc.tensor.matmul(ps[:, BANK_Y, :], ident[:], hc[:, 2 * half + q, :], start=False, stop=False)
                last.then_inc(summed, 1)

            def body(k, i):
                for half in range(2):
                    g = k * N // 2 + BODY // 2 * i + half
                    for q in (2 * half, 2 * half + 1):
                        n = k * N + BODY * i + q
                        wait(pe, b_used, n - 1)
                        nc.tensor.matmul(ps[:, BANK_B + q % 2, :],
                                         sel_row[:, bass.ds(BODY * i + q, 1)].broadcast_to([6 * N, D]),
                                         bc[:, k, :], start=True, stop=True).then_inc(b_ready, 1)
                    wait(pe, c_kept, g)
                    for q in (2 * half, 2 * half + 1):
                        last = nc.tensor.matmul(ps[:, BANK_C + q % 2, :],
                                                sel_row[:, bass.ds(N + BODY * i + q, 1)].broadcast_to([6 * N, D]),
                                                bc[:, k, :], start=True, stop=True)
                    last.then_inc(c_ready, 1)
                    if not (isinstance(i, int) and i == 0 and k == 0):
                        sum_states(half, g - 2)

            dt_product(0)
            pe.wait_ge(diag_ready, K)
            pe.wait_ge(u_ready, K)
            skip(0)
            skip(1)
            skip(2)
            pe.wait_ge(proj_kept, K)
            pe.wait_ge(bc_ready, 2)
            for k in states_loop(nc.tensor, body):
                if k + 1 < K:
                    dt_product(k + 1)
                if k:
                    pe.wait_ge(bc_ready, 2 * (k + 1))
            sum_states(0, K * N // 2 - 2)
            sum_states(1, K * N // 2 - 1)
            nc.tensor.matmul(ps[:, BANK_Y, :], d_diag[:, K - 1, :], u[:, K - 1, :], start=False,
                             stop=True).then_inc(y_ready, 1)

            pe.wait_ge(yg_ready, 1)
            pe.wait_ge(out_in, 16)
            for t in range(NT):
                last = nc.tensor.matmul(ps[:, 0, t * C:(t + 1) * C], yg[:, t * P:(t + 1) * P], w_out[:], start=True, stop=True)
            last.then_inc(op_ready, 1)

            pe.wait_ge(tn_ready, 1)
            for t in range(NT):
                last = nc.tensor.matmul(ps[0:C, 1, t * P:(t + 1) * P], tn[:, t, :], ident[:], start=True, stop=True)
            last.then_inc(tnT_ready, 1)
            pe.wait_ge(tnT_kept, 2)
            pe.wait_ge(qkv_in, 32)
            for j in range(2):
                nc.tensor.matmul(ps[0:C, 2 + j, :], wqkv[:, j, :], tnT[:], start=True, stop=True).then_inc(qk_ready, 1)
            for t in range(NT):
                last = nc.tensor.matmul(ps[:, 4, t * C:(t + 1) * C], tnT[:, t * P:(t + 1) * P], wqkv[:, 2, :], start=True, stop=True)
            last.then_inc(v_ready, 1)
            pe.wait_ge(q_kept, 1)
            pe.wait_ge(k_kept, 1)
            for b in range(B):
                for t in (2 * b, 2 * b + 1):
                    last = nc.tensor.matmul(ps[:, 5 + b, (t % 2) * L:(t % 2 + 1) * L], qT[:, t * P:(t + 1) * P],
                                            kT[:, b * L:(b + 1) * L], start=True, stop=True)
                last.then_inc(s_ready, 1)
            for t in range(NT):
                pe.wait_ge(pr_ready, t + 1)
                for kt in range(2):
                    at = ((t % 2) * 2 + kt) * P
                    last = nc.tensor.matmul(ps[:, t // 2, at:at + P], pr[:, t, kt * P:(kt + 1) * P], ident[:], start=True, stop=True)
                if t % 2:
                    last.then_inc(prT_ready, 1)
            pe.wait_ge(v_kept, 1)
            pe.wait_ge(prT_kept_a, 1)
            pe.wait_ge(prT_kept_d, 1)
            for t in range(NT):
                for kt in range(2):
                    last = nc.tensor.matmul(ps[:, 7, t * C:(t + 1) * C], prT[:, t, kt, :], v[:, 2 * (t // 2) + kt, :],
                                            start=(kt == 0), stop=(kt == 1))
            last.then_inc(o_ready, 1)

            pe.wait_ge(tn_ready, 2)
            for t in range(NT):
                last = nc.tensor.matmul(ps[:, 2, t * P:(t + 1) * P],
                                        tn2[:, t].rearrange("p a c -> p (a c)"), ident[:], start=True, stop=True)
            last.then_inc(fT_ready, 1)
            pe.wait_ge(fT_kept, 1)
            for t in range(NT):
                nc.tensor.matmul(ps[:, 7, t * E:(t + 1) * E], fT[0:C, t * P:(t + 1) * P], w_rt[:], start=True,
                                 stop=True).then_inc(down_done if t < 2 else lo_ready, 1)

            with nc.tensor.Fori(0, PAIRS // 2) as it:
                def ups(half, s):
                    S = 2 * STEPS * it + STEPS * half + s
                    j, e = s // 2, s % 2
                    rows = HW if j < HT - 1 else HID - (HT - 1) * HW
                    pe.wait_ge(glu_ready, S + 1)
                    for which in range(2):
                        for part, rest in ((fh, False), (fl, True)):
                            last = nc.tensor.matmul(ps[0:rows, BANK_H + 2 * (s % 3) + which, :],
                                                    wup[:, half, e, which, j * HW:j * HW + rows], part[:],
                                                    start=not rest, stop=rest)
                    last.then_inc(up_ready, 1)

                def downs(half, j):
                    rows = HW if j < HT - 1 else HID - (HT - 1) * HW
                    pe.wait_ge(glu_ready, 2 * STEPS * it + STEPS * half + 2 * j + 2 + 3)
                    if j == 0:
                        pe.wait_ge(y_added, 4 * it + 1)
                    for e in range(2):
                        last = nc.tensor.matmul(ps[e * C:(e + 1) * C, BANK_O + half, :], wdn[0:rows, half, e, j, :],
                                                gl[0:rows, (2 * j + e) % 4, :], start=(j == 0), stop=(j == HT - 1))
                    last.then_inc(down_done, 1)

                def turn_pair(half):
                    pe.wait_ge(y_kept, 2 * it + half + 1)
                    for t in range(NT):
                        last = nc.tensor.matmul(ps[:, BANK_O + half, t * P:(t + 1) * P], ysb[:, t * P:(t + 1) * P],
                                                ident[:], start=True, stop=True)
                    last.then_inc(yT_ready, 1)

                for half in range(2):
                    pe.wait_ge(slot_ready[half], 16 * it + 1)
                    pe.wait_ge(down_in[half], 64 * it + 64)
                    for s in range(STEPS):
                        ups(half, s)
                        if s >= 3 and s % 2:
                            downs(half, (s - 3) // 2)
                        if half and s == 1:
                            downs(0, HT - 1)
                        if half and s == 4:
                            turn_pair(0)
                downs(1, HT - 1)
                turn_pair(1)


def kernel(**inputs):
    import numpy as _np
    import concourse.bacc as _bacc
    from concourse import mybir as _mybir
    from concourse.bass_utils import run_bass_kernel_spmd as _run

    i = {n: _np.asarray(a) for n, a in inputs.items()}
    x = i["x"]
    tok = x.reshape(T, C)
    cw = i["L0_conv_conv_w"]
    laid = {
        "x_grp": x.reshape(B, L, G, 2).transpose(0, 2, 3, 1).reshape(B * G, 2 * L),
        "x_chan": tok.T,
        "x_tok": tok.reshape(NT, P, C).transpose(1, 0, 2),
        "in_proj": i["L0_conv_in_proj_w"],
        "conv_w": cw.transpose(1, 2, 3, 0).reshape(D, TAPS, D),
        "conv_b": i["L0_conv_conv_b"].reshape(D, 1),
        "xproj": i["L0_conv_xproj_w"].T.reshape(D, K // 2, 2 * R + 4 * N),
        "dt_wb": _np.concatenate([i["L0_conv_dt_w"].transpose(2, 0, 1), i["L0_conv_dt_b"][None]], axis=0),
        "a_logs": i["L0_conv_A_logs"].transpose(1, 0, 2).reshape(D, K * N),
        "d_skip": i["L0_conv_Ds"].T,
        "out_proj": i["L0_conv_out_proj_w"],
        "w_qkv": _np.stack([_np.concatenate([i[f"L1_attn_W{n}"].T, i[f"L1_attn_b{n}"][None]], axis=0) for n in "qkv"], axis=1),
        "w_router": i["L1_ffn_router_w"].T,
        "w_up": _np.stack([i["L1_ffn_w1"].transpose(2, 0, 1), i["L1_ffn_w3"].transpose(2, 0, 1)], axis=2),
        "w_down": i["L1_ffn_w2"].transpose(0, 2, 1),
    }
    nc = _bacc.Bacc("TRN2", target_bir_lowering=False, num_devices=1)
    arrays, args = {}, []
    for name, a in laid.items():
        a = _np.ascontiguousarray(a)
        arrays[f"{name}_dram"] = a
        args.append(nc.dram_tensor(f"{name}_dram", a.shape, _mybir.dt.from_np(a.dtype), kind="ExternalInput").ap())
    args.append(nc.dram_tensor("out_dram", (P, NT, C), _mybir.dt.float32, kind="ExternalOutput").ap())
    hybrid_kernel(nc, *args)
    r = _run(nc, [arrays], core_ids=[0])
    return _np.asarray(r.results[0]["out_dram"]).transpose(1, 0, 2).reshape(B, H, W, C)
```

```python
import concourse.bass as bass
from concourse import mybir
from contextlib import ExitStack

FP32 = mybir.dt.float32
BF16 = mybir.dt.bfloat16
FP32R = mybir.dt.float32r
ALU = mybir.AluOpType
ACT = mybir.ActivationFunctionType
AX = mybir.AxisListType

B, H, W, C = 2, 16, 16, 64
L = H * W
T = B * L
P = 128
NT = T // P
D = 2 * C
N = 16
R = 16
K = 4
G = 32
E = 8
HID = 682
HT = -(-HID // P)
HW = -(-HID // HT)
BODY = 4
LAG = 4
PAIRS = E // 2
STEPS = 2 * HT
TAPS = 9
WARM_UP = 15
W1, W2, W4, W5, W6, W7 = 3, 12, 2, 8, 16, 4
REACH = 3
WIN = P + 4
NEG = -1.0e30


def hybrid_kernel(nc, x_grp, x_chan, x_tok, in_proj, conv_w, conv_b, xproj, dt_wb, a_logs, d_skip,
                  out_proj, w_qkv, w_router, w_up, w_down, out):
    ctx = ExitStack()
    with ctx:
        def sb(name, shape, dt=FP32):
            return ctx.enter_context(nc.sbuf_tensor(name, shape, dt))

        def sem(name):
            return ctx.enter_context(nc.semaphore(name))

        ps = ctx.enter_context(nc.psum_tensor("ps", [P, 8, 512], FP32))

        xg = sb("xg", [B * G, 2 * L])
        xc = sb("xc", [C, T])
        xt = sb("xt", [P, NT, C])
        w_in = sb("w_in", [C, 2 * D])
        w_conv = sb("w_conv", [D, TAPS, D])
        b_conv = sb("b_conv", [D, 1])
        w_xp = sb("w_xp", [D, K // 2, 2 * R + 4 * N])
        w_rep = sb("w_rep", [D, K, 3 * 2 * N])
        w_dt = sb("w_dt", [2 * R + 1, K, D])
        a_log = sb("a_log", [D, K * N])
        a_exp = sb("a_exp", [D, K * N])
        a_neg = sb("a_neg", [D, K * N])
        dsk = sb("dsk", [D, K])
        w_out = sb("w_out", [D, C])
        wqkv = sb("wqkv", [C + 1, 3, C])
        w_rt = sb("w_rt", [C, E])
        wraw = sb("wraw", [2 * C, 2, 2, 2, HID])
        wup = sb("wup", [2 * C, 2, 2, 2, HID], FP32R)
        wdn = sb("wdn", [P, 2, 2, HT, C])

        ident = sb("ident", [P, P])
        flip = sb("flip", [D, D])
        sel_row = sb("sel_row", [3 * 2 * N, 2 * N], BF16)
        sel_grp = sb("sel_grp", [B * G, B, G, 2])
        band = sb("band", [P, 2, WIN])
        rank = sb("rank", [P, E])

        st_g = sb("st_g", [B * G, 6])
        mr_g = sb("mr_g", [B * G, 2])
        sd_g = sb("sd_g", [B * G, 1])
        mr_c = sb("mr_c", [C, B, 2])
        xn = sb("xn", [C, T])
        xpad = sb("xpad", [D, B, H + 2, W + 2])
        zs = sb("zs", [D, T])
        u = sb("u", [D, K, T])
        d_diag = sb("d_diag", [D, K, D])
        dtr = sb("dtr", [2 * R + 1, K // 2, T])
        bc = sb("bc", [3 * 2 * N, 2, T], BF16)
        minus = sb("minus", [3 * 2 * N, 2 * 3 * 2 * N], BF16)
        ex = sb("ex", [D, 2, T])
        lg = sb("lg", [D, 2, T])
        cr = sb("cr", [D, T])
        delta = sb("delta", [D, 2, T])
        du = sb("du", [D, 2, T])
        bdu = sb("bdu", [D, 2, T])
        rings = sb("rings", [D, 4, BODY * T])
        da = rings[:, 0].rearrange("p (q b l) -> p q b l", q=BODY, b=B)
        hs, cs, hc = (rings[:, r].rearrange("p (q t) -> p q t", q=BODY) for r in (1, 2, 3))
        wnext = rings[:].rearrange("p r n -> p (r n)")[:, 0:2 * 4 * HID].bitcast(FP32R).rearrange(
            "p (s a b h) -> p s a b h", s=2, a=2, b=2)
        yg = sb("yg", [D, T])

        t1 = sb("t1", [P, NT, C])
        t2 = sb("t2", [P, NT, C])
        st = sb("st", [P, NT, 6])
        mv = sb("mv", [P, NT, 2])
        sd = sb("sd", [P, NT])
        rs = sb("rs", [P, NT])
        dm = sb("dm", [P, NT, C])
        tn = sb("tn", [P, NT, C])
        tn2 = sb("tn2", [P, NT, 2, C])
        tnT = sb("tnT", [C + 1, T])
        qT = sb("qT", [C, T])
        kT = sb("kT", [C, T])
        v = sb("v", [P, NT, C])
        sc = sb("sc", [P, NT, WIN])
        mx = sb("mx", [P, NT])
        eps = sb("eps", [P, 1])
        nm = sb("nm", [P, NT])
        pr = sb("pr", [P, NT, L])
        sums = sb("sums", [P, NT])
        rsum = sb("rsum", [P, NT])
        prT = sb("prT", [P, NT, 2, P])
        ov = sb("ov", [P, NT, C])
        fT = sb("fT", [C, T])
        fh = sb("fh", [P, T], FP32R)
        fl = sb("fl", [P, T], FP32R)

        lo = sb("lo", [P, NT, E])
        le = sb("le", [P, NT, E])
        pb = sb("pb", [P, NT, E])
        g1 = sb("g1", [P, NT])
        g2 = sb("g2", [P, NT])
        g3 = sb("g3", [P, NT])
        m1 = sb("m1", [P, NT])
        m2 = sb("m2", [P, NT])
        key = sb("key", [P, NT, E])
        oh1 = sb("oh1", [P, NT, E])
        oh2 = sb("oh2", [P, NT, E])
        pb2 = sb("pb2", [P, NT, E])
        gate = sb("gate", [P, NT, E])
        si = sb("si", [P, 2, T])
        gl = sb("gl", [P, 4, T])
        ysb = sb("ysb", [P, T])
        gy = sb("gy", [P, NT, 2, C])
        acc = sb("acc", [P, NT, 2, C])
        res = sb("res", [P, NT, C])
        warm = gl[:, 0, 0:T // 2].bitcast(BF16)

        x_in, xc_in, xt_in, win_in, conv_in, prm_in, qkv_in, out_in = (
            sem(n) for n in ("x_in", "xc_in", "xt_in", "win_in", "conv_in", "prm_in", "qkv_in", "out_in"))
        raw_in = [sem(f"raw_in{i}") for i in range(2)]
        down_in = [sem(f"down_in{i}") for i in range(2)]
        slot_ready = [sem(f"slot_ready{i}") for i in range(2)]
        w_rounded, w_split, fT_kept = (sem(n) for n in ("w_rounded", "w_split", "fT_kept"))
        stored = sem("stored")
        pool_step = sem("pool_step")
        dve_step = sem("dve_step")
        warm_set = sem("warm_set")
        dt_zero = sem("dt_zero")
        pad_zero = sem("pad_zero")
        dtr_set = sem("dtr_set")
        da_zero = sem("da_zero")
        sd_ready, mr_ready, mrc_ready, mrc_copied, xn_ready = (
            sem(n) for n in ("sd_ready", "mr_ready", "mrc_ready", "mrc_copied", "xn_ready"))
        flip_ready = sem("flip_ready")
        xi_ready, xi_padded, conv_ready, u_ready, z_done = (
            sem(n) for n in ("xi_ready", "xi_padded", "conv_ready", "u_ready", "z_done"))
        dtr_ready, dtr_kept, proj_ready, rest_ready, part_kept = (
            sem(n) for n in ("dtr_ready", "dtr_kept", "proj_ready", "rest_ready", "part_kept"))
        aexp_ready, aneg_ready, diag_ready = (sem(n) for n in ("aexp_ready", "aneg_ready", "diag_ready"))
        dt_ready, abs_ready, ex_ready, log_ready, delta_ready, du_ready = (
            sem(n) for n in ("dt_ready", "abs_ready", "ex_ready", "log_ready", "delta_ready", "du_ready"))
        b_ready, b_used, c_ready, c_kept, da_ready, scanned, weighted, summed = (
            sem(n) for n in ("b_ready", "b_used", "c_ready", "c_kept", "da_ready", "scanned",
                             "weighted", "summed"))
        y_ready, yg_ready, op_ready = (sem(n) for n in ("y_ready", "yg_ready", "op_ready"))
        var_ready, sdt_ready, tn_ready, tnT_ready, tnT_kept = (
            sem(n) for n in ("var_ready", "sdt_ready", "tn_ready", "tnT_ready", "tnT_kept"))
        qk_ready, v_ready, q_kept, k_kept, v_kept, s_ready, mx_ready, pr_ready = (
            sem(n) for n in ("qk_ready", "v_ready", "q_kept", "k_kept", "v_kept", "s_ready",
                             "mx_ready", "pr_ready"))
        prT_ready, prT_kept_a, prT_kept_d, o_ready = (
            sem(n) for n in ("prT_ready", "prT_kept_a", "prT_kept_d", "o_ready"))
        fT_ready, lo_ready, lsub_ready, le_ready = (
            sem(n) for n in ("fT_ready", "lo_ready", "lsub_ready", "le_ready"))
        up_ready, silu_ready, glu_ready, down_done, y_kept, yT_ready, y_added, res_ready = (
            sem(n) for n in ("up_ready", "silu_ready", "glu_ready", "down_done", "y_kept", "yT_ready",
                             "y_added", "res_ready"))

        block = ctx.enter_context(nc.Block())

        def wait(eng, s, value):
            if isinstance(value, int) and value <= 0:
                return
            eng.wait_ge(s, value)

        def states_loop(eng, body):
            for k in range(K):
                body(k, 0)
                with eng.Fori(1, N // BODY - 1) as i:
                    body(k, i)
                body(k, N // BODY - 1)

        BANK_B, BANK_XP, BANK_C, BANK_Y, BANKS_DT = 0, 2, 4, 6, (7, 3)
        BANKS_DTR = (5, 1)
        BANK_WARM = 4
        PRM_IN = 16 * 7
        BANK_H, BANK_O = 0, 6

        @block.sync
        def _(sp):
            sp.dma_start(xg[:], x_grp).then_inc(x_in, 16)
            sp.dma_start(xc[:], x_chan).then_inc(xc_in, 16)
            sp.dma_start(w_in[:], in_proj).then_inc(win_in, 16)
            sp.dma_start(w_conv[:], conv_w).then_inc(conv_in, 16)
            sp.dma_start(w_xp[:], xproj).then_inc(prm_in, 16)
            sp.dma_start(b_conv[:], conv_b).then_inc(prm_in, 16)
            sp.dma_start(a_log[:], a_logs).then_inc(prm_in, 16)
            sp.dma_start(dsk[:], d_skip).then_inc(prm_in, 16)
            sp.wait_ge(dt_zero, 1)
            for odd in range(2):
                sp.dma_start(w_dt[odd * R:(odd + 1) * R].rearrange("r (h o) d -> r h o d", o=2)[:, :, odd],
                             dt_wb[0:R].rearrange("r (h o) d -> r h o d", o=2)[:, :, odd]).then_inc(prm_in, 16)
            sp.dma_start(w_dt[2 * R:2 * R + 1], dt_wb[R:R + 1]).then_inc(prm_in, 16)
            sp.dma_start(xt[:], x_tok).then_inc(xt_in, 16)
            sp.dma_start(w_out[:], out_proj).then_inc(out_in, 16)
            sp.dma_start(wqkv[:], w_qkv).then_inc(qkv_in, 16)
            sp.dma_start(w_rt[:], w_router).then_inc(qkv_in, 16)
            def load_raw(pair):
                for half in range(2):
                    sp.dma_start(wraw[half * C:(half + 1) * C, pair % 2],
                                 w_up[:, 2 * pair:2 * pair + 2]).then_inc(raw_in[pair % 2], 16)

            def load_down(pair):
                for e in range(2):
                    sp.dma_start(wdn[0:HW, pair % 2, e, 0:HT - 1, :],
                                 w_down[2 * pair + e, 0:(HT - 1) * HW, :].rearrange("(j p) c -> p j c", p=HW)
                                 ).then_inc(down_in[pair % 2], 16)
                    sp.dma_start(wdn[0:HID - (HT - 1) * HW, pair % 2, e, HT - 1, :],
                                 w_down[2 * pair + e, (HT - 1) * HW:HID, :]).then_inc(down_in[pair % 2], 16)

            for pair in range(2):
                load_raw(pair)
                load_down(pair)
            for pair in range(2, PAIRS):
                sp.wait_ge(slot_ready[pair % 2], 1)
                load_raw(pair)
            for pair in range(2, PAIRS):
                sp.wait_ge(w_split, pair - 1)
                sp.wait_ge(up_ready, STEPS * (pair - 1))
                sp.dma_start(wup[:, pair % 2].rearrange("p a b h -> p (a b h)").bitcast(FP32),
                             wnext[:, pair % 2].rearrange("p a b h -> p (a b h)").bitcast(FP32)).then_inc(slot_ready[pair % 2], 16)
                sp.wait_ge(down_done, 2 + HT * (pair - 1))
                load_down(pair)
            sp.wait_ge(res_ready, 1)
            sp.dma_start(out, res[:]).then_inc(stored, 16)
            sp.wait_ge(stored, 16)

        @block.gpsimd
        def _(pool):
            done = [0]

            def step(ins):
                done[0] += 1
                ins.then_inc(pool_step, 1)

            def wait_steps():
                pool.wait_ge(pool_step, done[0])

            step(nc.gpsimd.memset(sel_grp[:], 0.0))
            step(nc.gpsimd.memset(ident[:], 0.0))
            step(nc.gpsimd.memset(sel_row[:], 0.0))
            step(nc.gpsimd.memset(flip[:], 0.0))
            step(nc.gpsimd.memset(minus[:], 0.0))
            wait_steps()
            step(nc.gpsimd.affine_select(out=sel_grp[:], in_=sel_grp[:], compare_op=ALU.not_equal, fill=1.0,
                                         base=0, pattern=[[-G, B], [-1, G], [0, 2]], channel_multiplier=1))
            step(nc.gpsimd.affine_select(out=ident[:], in_=ident[:], compare_op=ALU.not_equal, fill=1.0,
                                         base=0, pattern=[[-1, P]], channel_multiplier=1))
            step(nc.gpsimd.affine_select(out=flip[:], in_=flip[:], compare_op=ALU.not_equal, fill=1.0,
                                         base=1 - D, pattern=[[1, D]], channel_multiplier=1))
            for part in range(3):
                wait_steps()
                step(nc.gpsimd.affine_select(out=sel_row[:], in_=sel_row[:], compare_op=ALU.not_equal, fill=1.0,
                                             base=-2 * N * part, pattern=[[-1, 2 * N]], channel_multiplier=1))
            wait_steps()
            step(nc.gpsimd.affine_select(out=minus[:], in_=minus[:], compare_op=ALU.not_equal, fill=-1.0,
                                         base=0, pattern=[[0, 2], [-1, 6 * N]], channel_multiplier=1))
            wait_steps()
            step(nc.gpsimd.affine_select(out=minus[:], in_=minus[:], compare_op=ALU.is_ge, fill=0.0,
                                         base=-2 * N, pattern=[[-2 * N, 2], [0, 6 * N]], channel_multiplier=1))
            pool.wait_ge(prm_in, PRM_IN)
            for k in range(K):
                half, odd = k // 2, k % 2
                for col, row in [(0, 2 * R + N * odd), (N, 2 * R + 2 * N + N * odd)]:
                    for copy in range(3):
                        at = col + 2 * N * copy
                        step(nc.gpsimd.tensor_copy(w_rep[:, k, at:at + N], w_xp[:, half, row:row + N]))
            step(nc.gpsimd.memset(band[:], 0.0))
            step(nc.gpsimd.iota(rank[:], pattern=[[-1, E]], base=E, channel_multiplier=0,
                                allow_small_or_imprecise_dtypes=True))
            for sign in (1, -1):
                wait_steps()
                step(nc.gpsimd.affine_select(out=band[:], in_=band[:], compare_op=ALU.is_ge, fill=NEG, base=REACH,
                                             pattern=[[sign * (L - WIN - P), 2], [sign, WIN]], channel_multiplier=-sign))
            step(nc.gpsimd.memset(pr[:], 0.0))
            step(nc.gpsimd.memset(eps[:], 1e-5))

            def body(k, i):
                for q in range(BODY):
                    n = k * N + BODY * i + q
                    wait(pool, scanned, n + 1)
                    if q % 2 == 0:
                        wait(pool, c_kept, k * N // 2 + BODY // 2 * i + q // 2 + 1)
                    wait(pool, summed, n - BODY + 1)
                    nc.gpsimd.tensor_tensor(hc[:, q], hs[:, q], cs[:, q], ALU.mult).then_inc(weighted, 1)

            states_loop(nc.gpsimd, body)

            pool.wait_ge(weighted, K * N)
            for pair in range(PAIRS):
                to = wup if pair < 2 else wnext
                pool.wait_ge(raw_in[pair % 2], 32 * (pair // 2 + 1))
                if pair == 2:
                    pool.wait_ge(y_ready, 1)
                if pair >= 2:
                    nc.gpsimd.tensor_copy(to[:, pair % 2], wraw[:, pair % 2]).then_inc(w_rounded, 1)
                pool.wait_ge(w_rounded, pair + 1)
                nc.gpsimd.tensor_tensor(to[C:2 * C, pair % 2], wraw[C:2 * C, pair % 2],
                                        to[C:2 * C, pair % 2].bitcast(FP32), ALU.subtract
                                        ).then_inc(slot_ready[pair] if pair < 2 else w_split, 1)
                if pair < 2:
                    pool.wait_ge(slot_ready[pair], 1)
                else:
                    pool.wait_ge(w_split, pair - 1)

        @block.scalar
        def _(act):
            nc.scalar.preload_act_table_set("sqrt_and_others")
            act.wait_ge(dve_step, 3)
            nc.scalar.activation(sd_g[:], mr_g[:, 1:2], ACT.Sqrt).then_inc(sd_ready, 1)
            nc.scalar.preload_act_table_set("silu_and_others")
            act.wait_ge(xi_ready, 1)
            act.wait_ge(pad_zero, 1)
            for b in range(B):
                last = nc.scalar.activation(xpad[:, b, 1:H + 1, 1:W + 1],
                                            ps[:, 0, b * L:(b + 1) * L].rearrange("p (h w) -> p h w", h=H), ACT.Copy)
                last.then_inc(xi_padded, 1)
            act.wait_ge(xi_ready, 2)
            nc.scalar.activation(zs[:], ps[:, 1, :], ACT.Silu).then_inc(z_done, 1)
            act.wait_ge(prm_in, PRM_IN)
            act.wait_ge(conv_ready, 1)
            nc.scalar.activation(u[:, 0, :], ps[:, 2, :], ACT.Silu, bias=b_conv[:]).then_inc(u_ready, 1)

            def by_columns(ap, inner):
                return ap.rearrange(f"p (b {inner}) -> p b w h", b=B, h=H, w=W)

            nc.scalar.activation(by_columns(u[:, 2, :], "w h"), by_columns(ps[:, 2, :], "h w"), ACT.Silu,
                                 bias=b_conv[:]).then_inc(u_ready, 1)
            nc.scalar.preload_act_table_set("exp_and_others")
            nc.scalar.activation(a_exp[:], a_log[:], ACT.Exp).then_inc(aexp_ready, 1)

            def keep_dtr(half):
                act.wait_ge(dtr_ready, half + 1)
                nc.scalar.activation(dtr[0:2 * R, half, :], ps[0:2 * R, BANKS_DTR[half], :], ACT.Copy).then_inc(dtr_kept, 1)

            def keep_part(k, part):
                if isinstance(part, int) and part == 0:
                    act.wait_ge(proj_ready, k + 1)
                else:
                    act.wait_ge(rest_ready, 2 * k + part)
                nc.scalar.activation(bc[:, k % 2, :], ps[0:6 * N, BANK_XP if k else BANK_B, :], ACT.Copy).then_inc(part_kept, 1)

            def exp_part(k):
                act.wait_ge(dt_ready, k + 1)
                nc.scalar.activation(ex[:, k % 2, :], ps[:, BANKS_DT[k % 2], :], ACT.Abs).then_inc(abs_ready, 1)
                act.wait_ge(abs_ready, k + 1)
                nc.scalar.activation(ex[:, k % 2, :], ex[:, k % 2, :], ACT.Exp, scale=-1.0).then_inc(ex_ready, 1)

            def log_part(k):
                act.wait_ge(ex_ready, k + 1)
                nc.scalar.activation(lg[:, k % 2, :], ex[:, k % 2, :], ACT.Ln, bias=1.0).then_inc(log_ready, 1)

            keep_dtr(0)
            keep_part(0, 0)
            keep_dtr(1)
            exp_part(0)
            keep_part(0, 1)
            exp_part(1)
            nc.scalar.preload_act_table_set("natural_log")
            log_part(0)
            keep_part(0, 2)
            log_part(1)
            nc.scalar.preload_act_table_set("exp_and_others")

            def body(k, i):
                if isinstance(i, int) and i == 0:
                    act.wait_ge(delta_ready, k + 1)
                for q in range(BODY):
                    n = k * N + BODY * i + q
                    wait(act, scanned, n - BODY + 1)
                    col = BODY * i + q
                    nc.scalar.activation(da[:, q, :, 1:L],
                                         delta[:, k % 2, :].rearrange("p (b l) -> p b l", b=B)[:, :, 1:L], ACT.Exp,
                                         scale=a_neg[:, bass.ds(k * N + col, 1)]).then_inc(da_ready, 1)
                    if q % 2:
                        g = k * N // 2 + BODY // 2 * i + q // 2
                        two = slice(q - 1, q + 1)
                        act.wait_ge(c_ready, g + 1)
                        wait(act, weighted, k * N + BODY * i + q - BODY + 1)
                        nc.scalar.activation(cs[:, two], ps[:, BANK_C:BANK_C + 2, :], ACT.Copy).then_inc(c_kept, 1)
                    if k == 0 and isinstance(i, int) and i == 0 and q == 0:
                        act.wait_ge(flip_ready, 1)
                        nc.scalar.activation(u[:, 1, :], ps[:, BANK_XP, :], ACT.Copy).then_inc(u_ready, 1)
                        nc.scalar.activation(by_columns(u[:, 3, :], "w h"), by_columns(ps[:, BANK_XP, :], "h w"),
                                             ACT.Copy).then_inc(u_ready, 1)
                    if q == 2 and k + 1 < K and not (isinstance(i, int) and i == N // BODY - 1):
                        keep_part(k + 1, i)
                    if k == 1 and isinstance(i, int) and i == 0 and q in (0, 2):
                        exp_part(2 + q // 2)
                if k == 1 and isinstance(i, int) and i == 0:
                    nc.scalar.preload_act_table_set("natural_log")
                    log_part(2)
                    log_part(3)
                    nc.scalar.preload_act_table_set("exp_and_others")

            act.wait_ge(aneg_ready, 1)
            act.wait_ge(da_zero, 1)
            states_loop(nc.scalar, body)

            nc.scalar.preload_act_table_set("sqrt_and_others")
            act.wait_ge(var_ready, NT)
            nc.scalar.activation(sd[:], mv[:, :, 1], ACT.Sqrt, bias=eps[:]).then_inc(sdt_ready, 1)
            nc.scalar.preload_act_table_set("exp_and_others")
            act.wait_ge(tnT_ready, 2)
            nc.scalar.activation(tnT[0:C, L:T], ps[0:C, 3, 0:L], ACT.Copy).then_inc(tnT_kept, 1)
            act.wait_ge(qk_ready, 1)
            nc.scalar.activation(qT[:], ps[0:C, 0, :], ACT.Copy).then_inc(q_kept, 1)
            act.wait_ge(v_ready, 1)
            nc.scalar.activation(v[:], ps[:, 4, 0:NT * C].rearrange("p (t c) -> p t c", t=NT), ACT.Copy).then_inc(v_kept, 1)
            for t in range(NT):
                act.wait_ge(mx_ready, t // 2 + 1)
                first = (t % 2) * (L - WIN)
                nc.scalar.activation(pr[:, t, first:first + WIN], sc[:, t, :], ACT.Exp, bias=nm[:, t:t + 1], scale=C ** -0.5,
                                     accum_out=sums[:, t:t + 1]).then_inc(pr_ready, 1)
            nc.scalar.preload_act_table_set("sqrt_and_others")
            act.wait_ge(prT_ready, 2)
            nc.scalar.activation(prT[:, 2:4], ps[:, 1, :], ACT.Copy).then_inc(prT_kept_a, 1)
            act.wait_ge(var_ready, 2 * NT)
            nc.scalar.activation(sd[:], mv[:, :, 1], ACT.Sqrt, bias=eps[:]).then_inc(sdt_ready, 1)
            nc.scalar.preload_act_table_set("exp_and_others")
            act.wait_ge(fT_ready, 1)
            act.wait_ge(glu_ready, 3)
            nc.scalar.activation(fT[:], ps[0:C, 2, :], ACT.Copy).then_inc(fT_kept, 1)
            act.wait_ge(lsub_ready, 1)
            nc.scalar.activation(le[:], lo[:], ACT.Exp).then_inc(le_ready, 1)

            nc.scalar.preload_act_table_set("silu_and_others")
            with nc.scalar.Fori(0, PAIRS // 2) as it:
                for half in range(2):
                    for s in range(STEPS):
                        S = 2 * STEPS * it + STEPS * half + s
                        rows = HW if s // 2 < HT - 1 else HID - (HT - 1) * HW
                        act.wait_ge(up_ready, S + 1)
                        act.wait_ge(glu_ready, S + 2)
                        nc.scalar.activation(si[0:rows, s % 2, :], ps[0:rows, BANK_H + 2 * (s % 3), :],
                                             ACT.Silu).then_inc(silu_ready, 1)
                        if half == 1 and s == 3:
                            act.wait_ge(down_done, 2 + HT * (2 * it + 1))
                            nc.scalar.activation(ysb[:], ps[:, BANK_O, :], ACT.Copy).then_inc(y_kept, 1)
                act.wait_ge(down_done, 2 + HT * (2 * it + 2))
                act.wait_ge(yT_ready, 2 * it + 1)
                nc.scalar.activation(ysb[:], ps[:, BANK_O + 1, :], ACT.Copy).then_inc(y_kept, 1)

        @block.vector
        def _(dve):
            done = [0]

            def chain(ins):
                done[0] += 1
                ins.then_inc(dve_step, 1)
                dve.wait_ge(dve_step, done[0])

            nc.vector.memset(gl[:, 0, 0:T // 2], 0.0).then_inc(warm_set, 1)
            nc.vector.memset(w_dt[0:2 * R], 0.0).then_inc(dt_zero, 1)
            dve.wait_ge(x_in, 16)
            chain(nc.vector.bn_stats(st_g[:], xg[:]))
            chain(nc.vector.bn_aggr(mr_g[:], st_g[:]))
            chain(nc.vector.tensor_scalar(mr_g[:, 1:2], mr_g[:, 1:2], 1e-5, None, ALU.add))
            nc.vector.memset(xpad[:], 0.0).then_inc(pad_zero, 1)
            nc.vector.memset(dtr[2 * R:2 * R + 1], 1.0).then_inc(dtr_set, 1)
            nc.vector.memset(da[:, :, :, 0:1], 0.0).then_inc(da_zero, 1)
            nc.vector.memset(tnT[C:C + 1, :], 1.0).then_inc(tnT_kept, 1)
            dve.wait_ge(sd_ready, 1)
            nc.vector.reciprocal(mr_g[:, 1:2], sd_g[:]).then_inc(mr_ready, 1)
            dve.wait_ge(mrc_ready, 1)
            nc.vector.tensor_copy(mr_c[:], ps[0:C, 7, 0:2 * B].rearrange("p (b s) -> p b s", b=B)).then_inc(mrc_copied, 1)
            dve.wait_ge(mrc_copied, 1)
            dve.wait_ge(xc_in, 16)
            for b in range(B):
                last = nc.vector.tensor_scalar(xn[:, b * L:(b + 1) * L], xc[:, b * L:(b + 1) * L], mr_c[:, b, 0:1],
                                               mr_c[:, b, 1:2], ALU.subtract, ALU.mult)
                last.then_inc(xn_ready, 1)
            dve.wait_ge(prm_in, PRM_IN)
            dve.wait_ge(pool_step, 7)
            for k in range(K):
                nc.vector.tensor_scalar(d_diag[:, k, :], ident[:], dsk[:, k:k + 1], None,
                                        ALU.mult).then_inc(diag_ready, 1)
            dve.wait_ge(aexp_ready, 1)
            nc.vector.tensor_scalar(a_neg[:], a_exp[:], -1.0, None, ALU.mult).then_inc(aneg_ready, 1)

            def step(ins):
                done[0] += 1
                ins.then_inc(dve_step, 1)
                return done[0]

            def prepare(k, part, marks):
                if part == 0:
                    dve.wait_ge(ex_ready, k + 1)
                    marks["e"] = step(nc.vector.tensor_scalar(cr[:], ex[:, k % 2, :], 1.0, -1.0, ALU.add, ALU.add))
                elif part == 1:
                    dve.wait_ge(dve_step, marks["e"])
                    marks["rounding"] = step(nc.vector.tensor_tensor(cr[:], ex[:, k % 2, :], cr[:], ALU.subtract))
                elif part == 2:
                    dve.wait_ge(dve_step, marks["rounding"])
                    dve.wait_ge(log_ready, k + 1)
                    marks["log1p"] = step(nc.vector.tensor_tensor(cr[:], cr[:], lg[:, k % 2, :], ALU.add))
                else:
                    dve.wait_ge(dve_step, marks["log1p"])
                    nc.vector.scalar_tensor_tensor(delta[:, k % 2, :], ps[:, BANKS_DT[k % 2], :], 0.0, cr[:], ALU.max,
                                                   ALU.add).then_inc(delta_ready, 1)
                    dve.wait_ge(delta_ready, k + 1)
                    dve.wait_ge(u_ready, K if k else 1)
                    nc.vector.tensor_tensor(du[:, k % 2, :], delta[:, k % 2, :], u[:, k, :], ALU.mult).then_inc(du_ready, 1)

            def body(k, i):
                marks = {} if isinstance(i, int) and i == (0, N // BODY - 1, 0, -1)[k] else None
                if isinstance(i, int) and i == 0:
                    dve.wait_ge(du_ready, k + 1)

                def times_b(q):
                    n = k * N + BODY * i + q
                    dve.wait_ge(b_ready, n + 1)
                    wait(dve, scanned, n - 1)
                    nc.vector.tensor_tensor(bdu[:, q % 2, :], ps[:, BANK_B + q % 2, :], du[:, k % 2, :],
                                            ALU.mult).then_inc(b_used, 1)

                def scan(q):
                    n = k * N + BODY * i + q
                    dve.wait_ge(da_ready, n + 1)
                    dve.wait_ge(b_used, n + 1)
                    wait(dve, weighted, n - BODY + 1)
                    nc.vector.tensor_tensor_scan(hs[:, q, :], da[:, q].rearrange("p b l -> p (b l)"),
                                                 bdu[:, q % 2, :], 0.0, ALU.mult, ALU.add).then_inc(scanned, 1)

                times_b(0)
                for q in range(1, BODY):
                    times_b(q)
                    scan(q - 1)
                    if marks is not None:
                        prepare(k + 1, q - 1, marks)
                if marks is not None:
                    prepare(k + 1, BODY - 1, marks)
                scan(BODY - 1)
                if k == 2 and isinstance(i, int) and i in (0, 3):
                    pair = i // 3
                    dve.wait_ge(raw_in[pair], 32)
                    nc.vector.tensor_copy(wup[:, pair], wraw[:, pair]).then_inc(w_rounded, 1)

            first_marks = {}
            for part in range(BODY):
                prepare(0, part, first_marks)
            states_loop(nc.vector, body)

            dve.wait_ge(y_ready, 1)
            dve.wait_ge(z_done, 1)
            nc.vector.tensor_tensor(yg[:], ps[:, BANK_Y, :], zs[:], ALU.mult).then_inc(yg_ready, 1)
            dve.wait_ge(op_ready, 1)
            dve.wait_ge(xt_in, 16)

            def over(ap, n):
                return ap.unsqueeze(2).broadcast_to([P, NT, n])

            def layer_norm(src, turn):
                for t in range(NT):
                    last = step(nc.vector.bn_stats(st[:, t, :], src[:, t, :]))
                dve.wait_ge(dve_step, last)
                for t in range(NT):
                    aggregated = nc.vector.bn_aggr(mv[:, t, :], st[:, t, :])
                    aggregated.then_inc(var_ready, 1)
                dve.wait_ge(var_ready, NT * turn)
                chain(nc.vector.tensor_tensor(dm[:], src[:], over(mv[:, :, 0], C), ALU.subtract))
                dve.wait_ge(sdt_ready, turn)
                chain(nc.vector.reciprocal(rs[:], sd[:]))
                if turn == 1:
                    normed = nc.vector.tensor_tensor(tn[:], dm[:], over(rs[:], C), ALU.mult)
                else:
                    normed = nc.vector.tensor_tensor(tn2[:], dm[:].unsqueeze(2).broadcast_to([P, NT, 2, C]),
                                                     rs[:].unsqueeze(2).unsqueeze(3).broadcast_to([P, NT, 2, C]), ALU.mult)
                normed.then_inc(tn_ready, 1)

            chain(nc.vector.tensor_tensor(t1[:], xt[:], ps[:, 0, 0:NT * C].rearrange("p (t c) -> p t c", t=NT), ALU.add))
            layer_norm(t1, 1)
            dve.wait_ge(tnT_ready, 1)
            nc.vector.tensor_copy(tnT[0:C, 0:L], ps[0:C, 1, 0:L]).then_inc(tnT_kept, 1)
            dve.wait_ge(qk_ready, 2)
            nc.vector.tensor_copy(kT[:], ps[0:C, 2, :]).then_inc(k_kept, 1)
            for b in range(B):
                two = slice(2 * b, 2 * b + 2)
                dve.wait_ge(s_ready, b + 1)
                chain(nc.vector.tensor_tensor(sc[:, two, :],
                                              ps[:, 5 + b, 0:2 * WIN].rearrange("p (t l) -> p t l", t=2), band[:], ALU.add))
                chain(nc.vector.tensor_reduce(mx[:, two], sc[:, two, :], AX.X, ALU.max))
                nc.vector.tensor_scalar(nm[:, two], mx[:, two], -(C ** -0.5), None, ALU.mult).then_inc(mx_ready, 1)
            dve.wait_ge(prT_ready, 1)
            nc.vector.tensor_copy(prT[:, 0:2], ps[:, 0, :].rearrange("p (t k q) -> p t k q", t=2, k=2)).then_inc(prT_kept_d, 1)
            dve.wait_ge(pr_ready, NT)
            chain(nc.vector.reciprocal(rsum[:], sums[:]))
            dve.wait_ge(o_ready, 1)
            chain(nc.vector.tensor_tensor(ov[:], ps[:, 7, 0:NT * C].rearrange("p (t c) -> p t c", t=NT), over(rsum[:], C), ALU.mult))
            chain(nc.vector.tensor_tensor(t2[:], t1[:], ov[:], ALU.add))
            layer_norm(t2, 2)
            nc.vector.tensor_copy(acc[:, :, 0, :], t2[:]).then_inc(glu_ready, 1)
            nc.vector.memset(acc[:, :, 1, :], 0.0).then_inc(y_added, 1)
            dve.wait_ge(fT_ready, 1)
            nc.vector.tensor_copy(fh[:], ps[:, 2, :]).then_inc(glu_ready, 1)
            dve.wait_ge(glu_ready, 2)
            nc.vector.tensor_tensor(fl[:], ps[:, 2, :], fh[:].bitcast(FP32), ALU.subtract).then_inc(glu_ready, 1)

            dve.wait_ge(lo_ready, 2)
            lps = ps[:, 7, 0:NT * E].rearrange("p (t e) -> p t e", t=NT)
            chain(nc.vector.tensor_reduce(g1[:], lps, AX.X, ALU.max))
            nc.vector.tensor_tensor(lo[:], lps, over(g1[:], E), ALU.subtract).then_inc(lsub_ready, 1)
            dve.wait_ge(le_ready, 1)
            chain(nc.vector.tensor_reduce(g2[:], le[:], AX.X, ALU.add))
            chain(nc.vector.reciprocal(g3[:], g2[:]))
            chain(nc.vector.tensor_tensor(pb[:], le[:], over(g3[:], E), ALU.mult))
            ranks = rank[:].unsqueeze(1).broadcast_to([P, NT, E])

            def pick_largest(src, top, one_hot):
                chain(nc.vector.tensor_reduce(top[:], src[:], AX.X, ALU.max))
                chain(nc.vector.tensor_tensor(key[:], src[:], over(top[:], E), ALU.is_equal))
                chain(nc.vector.tensor_tensor(key[:], key[:], ranks, ALU.mult))
                chain(nc.vector.tensor_reduce(g1[:], key[:], AX.X, ALU.max))
                chain(nc.vector.tensor_tensor(one_hot[:], key[:], over(g1[:], E), ALU.is_equal))

            pick_largest(pb, m1, oh1)
            chain(nc.vector.scalar_tensor_tensor(pb2[:], oh1[:], -4.0, pb[:], ALU.mult, ALU.add))
            pick_largest(pb2, m2, oh2)
            chain(nc.vector.tensor_tensor(g2[:], m1[:], m2[:], ALU.add))
            chain(nc.vector.tensor_scalar(g2[:], g2[:], 1e-9, None, ALU.add))
            chain(nc.vector.reciprocal(g3[:], g2[:]))
            chain(nc.vector.tensor_tensor(oh1[:], oh1[:], oh2[:], ALU.add))
            chain(nc.vector.tensor_tensor(pb[:], pb[:], over(g3[:], E), ALU.mult))
            chain(nc.vector.tensor_tensor(gate[:], oh1[:], pb[:], ALU.mult))

            with nc.vector.Fori(0, PAIRS // 2) as it:
                def add_pair(half):
                    pair = 2 * it + half
                    dve.wait_ge(yT_ready, pair + 1)
                    g_ap = gate[:, :, bass.ds(2 * pair, 2)].unsqueeze(3).broadcast_to([P, NT, 2, C])
                    nc.vector.tensor_tensor(gy[:], ps[:, BANK_O + half, :].rearrange("p (t e c) -> p t e c", t=NT, e=2),
                                            g_ap, ALU.mult).then_inc(y_added, 1)
                    dve.wait_ge(y_added, 2 * pair + 2)
                    nc.vector.tensor_tensor(acc[:], acc[:], gy[:], ALU.add).then_inc(y_added, 1)
                    dve.wait_ge(y_added, 2 * pair + 3)

                for half in range(2):
                    for s in range(STEPS):
                        S = 2 * STEPS * it + STEPS * half + s
                        rows = HW if s // 2 < HT - 1 else HID - (HT - 1) * HW
                        dve.wait_ge(silu_ready, S + 1)
                        dve.wait_ge(down_done, STEPS * it + (STEPS * half + s) // 2 + 1)
                        nc.vector.tensor_tensor(gl[0:rows, s % 4, :], ps[0:rows, BANK_H + 2 * (s % 3) + 1, :],
                                                si[0:rows, s % 2, :], ALU.mult).then_inc(glu_ready, 1)
                        if half == 1 and s == 5:
                            add_pair(0)
                add_pair(1)
            nc.vector.tensor_tensor(res[:], acc[:, :, 0, :], acc[:, :, 1, :], ALU.add).then_inc(res_ready, 1)

        @block.tensor
        def _(pe):
            def keep_warm(count):
                for _ in range(count):
                    nc.tensor.matmul(ps[:, BANK_WARM, :], warm[:, 0:P], warm[:], start=True, stop=True)

            pe.wait_ge(warm_set, 1)
            keep_warm(WARM_UP)
            pe.wait_ge(mr_ready, 1)
            pe.wait_ge(pool_step, 6)
            for b in range(B):
                last = nc.tensor.matmul(ps[0:C, 7, 2 * b:2 * b + 2], sel_grp[:, b].rearrange("p g c -> p (g c)"),
                                        mr_g[:], start=True, stop=True)
            last.then_inc(mrc_ready, 1)
            pe.wait_ge(xn_ready, B)
            pe.wait_ge(win_in, 16)
            for half in range(2):
                nc.tensor.matmul(ps[:, half, :], w_in[:, half * D:(half + 1) * D], xn[:], start=True,
                                 stop=True).then_inc(xi_ready, 1)
            pe.wait_ge(xi_padded, B)
            pe.wait_ge(conv_in, 16)
            for tap in range(TAPS):
                last = nc.tensor.matmul(ps[:, 2, :], w_conv[:, tap, :],
                                        xpad[:, :, tap // 3:tap // 3 + H, tap % 3:tap % 3 + W],
                                        start=(tap == 0), stop=(tap == TAPS - 1))
            last.then_inc(conv_ready, 1)

            def dt_rows(half):
                nc.tensor.matmul(ps[0:2 * R, BANKS_DTR[half], :], w_xp[:, half, 0:2 * R], u[:, 2 * half, :], start=True,
                                 stop=True).then_inc(dtr_ready, 1)

            def project(k):
                nc.tensor.matmul(ps[0:6 * N, BANK_XP if k else BANK_B, :], w_rep[:, k, :], u[:, 2 * (k // 2), :], start=True,
                                 stop=True).then_inc(proj_ready, 1)

            def take_off(k, part):
                pe.wait_ge(part_kept, 3 * k + part)
                nc.tensor.matmul(ps[0:6 * N, BANK_XP if k else BANK_B, :], minus[:, bass.ds(6 * N * part - 6 * N, 6 * N)],
                                 bc[:, k % 2, :], start=False, stop=True, skip_group_check=True).then_inc(rest_ready, 1)

            def dt_product(k):
                if k > 1:
                    pe.wait_ge(delta_ready, k - 1)
                nc.tensor.matmul(ps[:, BANKS_DT[k % 2], :], w_dt[:, k, :], dtr[:, k // 2, :],
                                 start=True, stop=True).then_inc(dt_ready, 1)

            def skip(k):
                nc.tensor.matmul(ps[:, BANK_Y, :], d_diag[:, k, :], u[:, k, :], start=(k == 0), stop=False)

            def sum_state(q, n):
                wait(pe, weighted, n + 1)
                last_state = isinstance(n, int) and n == K * N - 1
                nc.tensor.matmul(ps[:, BANK_Y, :], ident[:], hc[:, q % BODY, :], start=False,
                                 stop=last_state).then_inc(y_ready if last_state else summed, 1)

            def body(k, i):
                peeled = i if isinstance(i, int) else None
                if peeled == 0:
                    pe.wait_ge(part_kept, 3 * (k + 1))
                for q in range(BODY):
                    n = k * N + BODY * i + q
                    wait(pe, b_used, n - 1)
                    nc.tensor.matmul(ps[:, BANK_B + q % 2, :],
                                     sel_row[:, bass.ds(BODY * i + q, 1)].broadcast_to([6 * N, D]),
                                     bc[:, k % 2, :], start=True, stop=True).then_inc(b_ready, 1)
                    if q % 2 == 0:
                        wait(pe, c_kept, k * N // 2 + BODY // 2 * i + q // 2)
                        for p in (q, q + 1):
                            last = nc.tensor.matmul(ps[:, BANK_C + p % 2, :],
                                                    sel_row[:, bass.ds(N + BODY * i + p, 1)].broadcast_to([6 * N, D]),
                                                    bc[:, k % 2, :], start=True, stop=True)
                        last.then_inc(c_ready, 1)
                    if not (isinstance(n, int) and n < LAG):
                        sum_state(q - LAG, n - LAG)
                    if q == 1 and k + 1 < K:
                        if peeled == 0:
                            if k == 0:
                                pe.wait_ge(u_ready, K)
                            project(k + 1)
                        elif peeled is None:
                            take_off(k + 1, i)
                    if peeled == N // BODY - 1:
                        if k == 0 and q < 2:
                            dt_product(2 + q)
                        if k in (1, 2) and q == 0:
                            skip(2 * k - 1)

            pe.wait_ge(u_ready, 1)
            pe.wait_ge(prm_in, PRM_IN)
            dt_rows(0)
            pe.wait_ge(pool_step, 13 + 6 * K)
            project(0)
            pe.wait_ge(u_ready, 2)
            pe.wait_ge(z_done, 1)
            dt_rows(1)
            pe.wait_ge(dtr_kept, 1)
            pe.wait_ge(dtr_set, 1)
            pe.wait_ge(mrc_copied, 1)
            dt_product(0)
            dt_product(1)
            take_off(0, 1)
            pe.wait_ge(diag_ready, K)
            nc.tensor.matmul(ps[:, BANK_XP, :], flip[:], u[:, 0, :], start=True, stop=True).then_inc(flip_ready, 1)
            skip(0)
            skip(2)
            take_off(0, 2)
            pe.wait_ge(dtr_kept, 2)
            states_loop(nc.tensor, body)
            for n in range(K * N - LAG, K * N):
                sum_state(n, n)

            keep_warm(W1)
            pe.wait_ge(yg_ready, 1)
            pe.wait_ge(out_in, 16)
            for t in range(NT):
                last = nc.tensor.matmul(ps[:, 0, t * C:(t + 1) * C], yg[:, t * P:(t + 1) * P], w_out[:], start=True, stop=True)
            last.then_inc(op_ready, 1)

            keep_warm(W2)
            pe.wait_ge(tn_ready, 1)
            for t in range(NT):
                last = nc.tensor.matmul(ps[0:C, 1 + 2 * (t // 2), (t % 2) * P:(t % 2 + 1) * P], tn[:, t, :], ident[:],
                                        start=True, stop=True)
                if t % 2:
                    last.then_inc(tnT_ready, 1)
            keep_warm(W4)
            pe.wait_ge(tnT_kept, 3)
            pe.wait_ge(qkv_in, 32)
            for j in range(2):
                nc.tensor.matmul(ps[0:C, 2 * j, :], wqkv[:, j, :], tnT[:], start=True, stop=True).then_inc(qk_ready, 1)
            for t in range(NT):
                last = nc.tensor.matmul(ps[:, 4, t * C:(t + 1) * C], tnT[:, t * P:(t + 1) * P], wqkv[:, 2, :], start=True, stop=True)
            last.then_inc(v_ready, 1)
            pe.wait_ge(q_kept, 1)
            pe.wait_ge(k_kept, 1)
            for b in range(B):
                for t in (2 * b, 2 * b + 1):
                    last = nc.tensor.matmul(ps[:, 5 + b, (t % 2) * WIN:(t % 2 + 1) * WIN], qT[:, t * P:(t + 1) * P],
                                            kT[:, b * L + (t % 2) * (L - WIN):b * L + (t % 2) * (L - WIN) + WIN], start=True, stop=True)
                last.then_inc(s_ready, 1)
            pe.wait_ge(v_kept, 1)
            keep_warm(W5)
            for t in range(NT):
                pe.wait_ge(pr_ready, t + 1)
                for kt in range(2):
                    at = ((t % 2) * 2 + kt) * P
                    last = nc.tensor.matmul(ps[:, t // 2, at:at + P], pr[:, t, kt * P:(kt + 1) * P], ident[:], start=True, stop=True)
                if t % 2:
                    last.then_inc(prT_ready, 1)
            pe.wait_ge(prT_kept_a, 1)
            pe.wait_ge(prT_kept_d, 1)
            for t in range(NT):
                for kt in range(2):
                    last = nc.tensor.matmul(ps[:, 7, t * C:(t + 1) * C], prT[:, t, kt, :], v[:, 2 * (t // 2) + kt, :],
                                            start=(kt == 0), stop=(kt == 1))
            last.then_inc(o_ready, 1)

            keep_warm(W6)
            pe.wait_ge(tn_ready, 2)
            for t in range(NT):
                last = nc.tensor.matmul(ps[:, 2, t * P:(t + 1) * P],
                                        tn2[:, t].rearrange("p a c -> p (a c)"), ident[:], start=True, stop=True)
            last.then_inc(fT_ready, 1)
            keep_warm(W7)
            pe.wait_ge(fT_kept, 1)
            for t in range(NT):
                nc.tensor.matmul(ps[:, 7, t * E:(t + 1) * E], fT[0:C, t * P:(t + 1) * P], w_rt[:], start=True,
                                 stop=True).then_inc(down_done if t < 2 else lo_ready, 1)

            with nc.tensor.Fori(0, PAIRS // 2) as it:
                def ups(half, s):
                    S = 2 * STEPS * it + STEPS * half + s
                    j, e = s // 2, s % 2
                    rows = HW if j < HT - 1 else HID - (HT - 1) * HW
                    pe.wait_ge(glu_ready, S + 1)
                    for which in range(2):
                        for part, rest in ((fh, False), (fl, True)):
                            last = nc.tensor.matmul(ps[0:rows, BANK_H + 2 * (s % 3) + which, :],
                                                    wup[:, half, e, which, j * HW:j * HW + rows], part[:],
                                                    start=not rest, stop=rest)
                    last.then_inc(up_ready, 1)

                def downs(half, j):
                    rows = HW if j < HT - 1 else HID - (HT - 1) * HW
                    pe.wait_ge(glu_ready, 2 * STEPS * it + STEPS * half + 2 * j + 2 + 3)
                    if j == 0:
                        pe.wait_ge(y_added, 4 * it + 1)
                    for e in range(2):
                        last = nc.tensor.matmul(ps[e * C:(e + 1) * C, BANK_O + half, :], wdn[0:rows, half, e, j, :],
                                                gl[0:rows, (2 * j + e) % 4, :], start=(j == 0), stop=(j == HT - 1))
                    last.then_inc(down_done, 1)

                def turn_pair(half):
                    pe.wait_ge(y_kept, 2 * it + half + 1)
                    for t in range(NT):
                        last = nc.tensor.matmul(ps[:, BANK_O + half, t * P:(t + 1) * P], ysb[:, t * P:(t + 1) * P],
                                                ident[:], start=True, stop=True)
                    last.then_inc(yT_ready, 1)

                for half in range(2):
                    pe.wait_ge(slot_ready[half], 16 * it + 1)
                    pe.wait_ge(down_in[half], 64 * it + 64)
                    for s in range(STEPS):
                        ups(half, s)
                        if s >= 3 and s % 2:
                            downs(half, (s - 3) // 2)
                        if half and s == 1:
                            downs(0, HT - 1)
                        if half and s == 4:
                            turn_pair(0)
                downs(1, HT - 1)
                turn_pair(1)


def kernel(**inputs):
    import numpy as _np
    import concourse.bacc as _bacc
    from concourse import mybir as _mybir
    from concourse.bass_utils import run_bass_kernel_spmd as _run

    i = {n: _np.asarray(a) for n, a in inputs.items()}
    x = i["x"]
    tok = x.reshape(T, C)
    cw = i["L0_conv_conv_w"]
    laid = {
        "x_grp": x.reshape(B, L, G, 2).transpose(0, 2, 3, 1).reshape(B * G, 2 * L),
        "x_chan": tok.T,
        "x_tok": tok.reshape(NT, P, C).transpose(1, 0, 2),
        "in_proj": i["L0_conv_in_proj_w"],
        "conv_w": cw.transpose(1, 2, 3, 0).reshape(D, TAPS, D),
        "conv_b": i["L0_conv_conv_b"].reshape(D, 1),
        "xproj": i["L0_conv_xproj_w"].T.reshape(D, K // 2, 2 * R + 4 * N),
        "dt_wb": _np.concatenate([i["L0_conv_dt_w"].transpose(2, 0, 1), i["L0_conv_dt_b"][None]], axis=0),
        "a_logs": i["L0_conv_A_logs"].transpose(1, 0, 2).reshape(D, K * N),
        "d_skip": i["L0_conv_Ds"].T,
        "out_proj": i["L0_conv_out_proj_w"],
        "w_qkv": _np.stack([_np.concatenate([i[f"L1_attn_W{n}"].T, i[f"L1_attn_b{n}"][None]], axis=0) for n in "qkv"], axis=1),
        "w_router": i["L1_ffn_router_w"].T,
        "w_up": _np.stack([i["L1_ffn_w1"].transpose(2, 0, 1), i["L1_ffn_w3"].transpose(2, 0, 1)], axis=2),
        "w_down": i["L1_ffn_w2"].transpose(0, 2, 1),
    }
    nc = _bacc.Bacc("TRN2", target_bir_lowering=False, num_devices=1)
    arrays, args = {}, []
    for name, a in laid.items():
        a = _np.ascontiguousarray(a)
        arrays[f"{name}_dram"] = a
        args.append(nc.dram_tensor(f"{name}_dram", a.shape, _mybir.dt.from_np(a.dtype), kind="ExternalInput").ap())
    args.append(nc.dram_tensor("out_dram", (P, NT, C), _mybir.dt.float32, kind="ExternalOutput").ap())
    hybrid_kernel(nc, *args)
    r = _run(nc, [arrays], core_ids=[0])
    return _np.asarray(r.results[0]["out_dram"]).transpose(1, 0, 2).reshape(B, H, W, C)
```

```python
import concourse.bass as bass
from concourse import mybir
from contextlib import ExitStack

FP32 = mybir.dt.float32
BF16 = mybir.dt.bfloat16
FP32R = mybir.dt.float32r
ALU = mybir.AluOpType
ACT = mybir.ActivationFunctionType
AX = mybir.AxisListType

B, H, W, C = 2, 16, 16, 64
L = H * W
T = B * L
P = 128
NT = T // P
D = 2 * C
N = 16
R = 16
K = 4
G = 32
E = 8
HID = 682
BODY = 4
LAG = 4
PAIRS = E // 2
STEPS = -(-2 * HID // P)
SHARED = HID // P
CUT = HID - SHARED * P
GROUPS = SHARED + 1
ORDER = [t for j in range(SHARED) for t in (j, SHARED + 1 + j)] + [SHARED]
BY_VECTOR = (0, 3)
TAPS = 9
WARM_UP = 10
REACH = 3
WIN = P + 4
NEG = -1.0e30


def hybrid_kernel(nc, x_grp, x_chan, x_tok, in_proj, conv_w, conv_b, xproj, dt_wb, a_logs, d_skip,
                  out_proj, w_qkv, w_router, w_up, w_down, out):
    ctx = ExitStack()
    with ctx:
        def sb(name, shape, dt=FP32):
            return ctx.enter_context(nc.sbuf_tensor(name, shape, dt))

        def sem(name):
            return ctx.enter_context(nc.semaphore(name))

        ps = ctx.enter_context(nc.psum_tensor("ps", [P, 8, 512], FP32))

        xg = sb("xg", [B * G, 2 * L])
        xc = sb("xc", [C, T])
        xt = sb("xt", [P, NT, C])
        w_in = sb("w_in", [C, 2 * D])
        w_conv = sb("w_conv", [D, TAPS, D])
        b_conv = sb("b_conv", [D, 1])
        w_xp = sb("w_xp", [D, K // 2, 2 * R + 4 * N])
        w_rep = sb("w_rep", [D, K, 3 * 2 * N])
        w_dt = sb("w_dt", [2 * R + 1, K, D])
        a_log = sb("a_log", [D, K * N])
        a_exp = sb("a_exp", [D, K * N])
        a_neg = sb("a_neg", [D, K * N])
        dsk = sb("dsk", [D, K])
        w_out = sb("w_out", [D, C])
        wqkv = sb("wqkv", [C + 1, 3, C])
        w_rt = sb("w_rt", [C, E])
        wraw = sb("wraw", [2 * C, 2, 2, 2, HID])
        wup = sb("wup", [2 * C, 2, 2, 2, HID], FP32R)
        wdn = sb("wdn", [P, 2, STEPS + 1, C])

        ident = sb("ident", [P, P])
        flip = sb("flip", [D, D])
        sel_row = sb("sel_row", [3 * 2 * N, 2 * N], BF16)
        sel_grp = sb("sel_grp", [B * G, B, G, 2])
        band = sb("band", [P, 2, WIN])
        rank = sb("rank", [P, E])

        st_g = sb("st_g", [B * G, 6])
        mr_g = sb("mr_g", [B * G, 2])
        sd_g = sb("sd_g", [B * G, 1])
        mr_c = sb("mr_c", [C, B, 2])
        xn = sb("xn", [C, T])
        xpad = sb("xpad", [D, B, H + 2, W + 2])
        zs = sb("zs", [D, T])
        u = sb("u", [D, K, T])
        d_cross = sb("d_cross", [D, K // 2, D])
        dtr = sb("dtr", [2 * R + 1, K // 2, T])
        bc = sb("bc", [3 * 2 * N, 2, T], BF16)
        minus = sb("minus", [3 * 2 * N, 2 * 3 * 2 * N], BF16)
        ex = sb("ex", [D, K, T])
        rd = sb("rd", [D, 3, T])
        delta = sb("delta", [D, 2, T])
        du = sb("du", [D, 2, T])
        bdu = sb("bdu", [D, 2, T])
        rings = sb("rings", [D, 4, BODY * T])
        da = rings[:, 0].rearrange("p (q b l) -> p q b l", q=BODY, b=B)
        hs, cs, hc = (rings[:, r].rearrange("p (q t) -> p q t", q=BODY) for r in (1, 2, 3))
        wnext = rings[:].rearrange("p r n -> p (r n)")[:, 0:2 * 4 * HID].bitcast(FP32R).rearrange(
            "p (s a b h) -> p s a b h", s=2, a=2, b=2)
        yg = sb("yg", [D, T])

        t1 = sb("t1", [P, NT, C])
        t2 = sb("t2", [P, NT, C])
        st = sb("st", [P, NT, 6])
        mv = sb("mv", [P, NT, 2])
        sd = sb("sd", [P, NT])
        rs = sb("rs", [P, NT])
        dm = sb("dm", [P, NT, C])
        tn = sb("tn", [P, NT, C])
        tn2 = sb("tn2", [P, NT, 2, C])
        tnT = sb("tnT", [C + 1, T])
        qT = sb("qT", [C, T])
        kT = sb("kT", [C, T])
        v = sb("v", [P, NT, C])
        sc = sb("sc", [P, NT, WIN])
        mx = sb("mx", [P, NT])
        eps = sb("eps", [P, 1])
        nm = sb("nm", [P, NT])
        pr = sb("pr", [P, NT, L])
        sums = sb("sums", [P, NT])
        rsum = sb("rsum", [P, NT])
        prT = sb("prT", [P, NT, 2, P])
        ov = sb("ov", [P, NT, C])
        fT = sb("fT", [C, T])
        fh = sb("fh", [P, T], FP32R)
        fl = sb("fl", [P, T], FP32R)

        lo = sb("lo", [P, NT, E])
        le = sb("le", [P, NT, E])
        pb = sb("pb", [P, NT, E])
        g1 = sb("g1", [P, NT])
        g2 = sb("g2", [P, NT])
        g3 = sb("g3", [P, NT])
        m1 = sb("m1", [P, NT])
        m2 = sb("m2", [P, NT])
        key = sb("key", [P, NT, E])
        oh1 = sb("oh1", [P, NT, E])
        oh2 = sb("oh2", [P, NT, E])
        pb2 = sb("pb2", [P, NT, E])
        gate = sb("gate", [P, NT, E])
        si = sb("si", [P, 2, T])
        gl = sb("gl", [P, 4, T])
        ysb = sb("ysb", [P, T])
        lg = [si[:, 0], si[:, 1], ysb[:], gl[:, 3]]
        above = {2: gl[:, 1], 3: gl[:, 2]}
        gy = sb("gy", [P, NT, 2, C])
        acc = sb("acc", [P, NT, 2, C])
        res = sb("res", [P, NT, C])
        warm = gl[:, 0, 0:T // 2].bitcast(BF16)

        x_in, xc_in, xt_in, win_in, conv_in, prm_in, qkv_in, out_in = (
            sem(n) for n in ("x_in", "xc_in", "xt_in", "win_in", "conv_in", "prm_in", "qkv_in", "out_in"))
        raw_in = [sem(f"raw_in{i}") for i in range(2)]
        down_in = [sem(f"down_in{i}") for i in range(2)]
        slot_ready = [sem(f"slot_ready{i}") for i in range(2)]
        w_rounded, w_split, fT_kept = (sem(n) for n in ("w_rounded", "w_split", "fT_kept"))
        stored = sem("stored")
        pool_step = sem("pool_step")
        dve_step = sem("dve_step")
        warm_set = sem("warm_set")
        dt_zero = sem("dt_zero")
        shared_zero = sem("shared_zero")
        pad_zero = sem("pad_zero")
        dtr_set = sem("dtr_set")
        rounding_ready = sem("rounding_ready")
        above_kept = sem("above_kept")
        da_zero = sem("da_zero")
        sd_ready, mr_ready, mrc_ready, mrc_copied, xn_ready = (
            sem(n) for n in ("sd_ready", "mr_ready", "mrc_ready", "mrc_copied", "xn_ready"))
        flip_ready = sem("flip_ready")
        xi_ready, xi_padded, conv_ready, u_ready, z_done = (
            sem(n) for n in ("xi_ready", "xi_padded", "conv_ready", "u_ready", "z_done"))
        dtr_ready, dtr_kept, proj_ready, rest_ready, part_kept = (
            sem(n) for n in ("dtr_ready", "dtr_kept", "proj_ready", "rest_ready", "part_kept"))
        aexp_ready, aneg_ready, diag_ready = (sem(n) for n in ("aexp_ready", "aneg_ready", "diag_ready"))
        dt_ready, abs_ready, ex_ready, log_ready, delta_ready, du_ready = (
            sem(n) for n in ("dt_ready", "abs_ready", "ex_ready", "log_ready", "delta_ready", "du_ready"))
        b_ready, b_used, c_ready, c_kept, da_ready, scanned, weighted, summed = (
            sem(n) for n in ("b_ready", "b_used", "c_ready", "c_kept", "da_ready", "scanned",
                             "weighted", "summed"))
        y_ready, yg_ready, op_ready = (sem(n) for n in ("y_ready", "yg_ready", "op_ready"))
        var_ready, sdt_ready, tn_ready, tnT_ready, tnT_kept = (
            sem(n) for n in ("var_ready", "sdt_ready", "tn_ready", "tnT_ready", "tnT_kept"))
        qk_ready, v_ready, q_kept, k_kept, v_kept, s_ready, mx_ready, pr_ready = (
            sem(n) for n in ("qk_ready", "v_ready", "q_kept", "k_kept", "v_kept", "s_ready",
                             "mx_ready", "pr_ready"))
        prT_ready, prT_kept_a, prT_kept_d, o_ready = (
            sem(n) for n in ("prT_ready", "prT_kept_a", "prT_kept_d", "o_ready"))
        fT_ready, lo_ready, lsub_ready, le_ready = (
            sem(n) for n in ("fT_ready", "lo_ready", "lsub_ready", "le_ready"))
        acc_set, f_split = sem("acc_set"), sem("f_split")
        up_ready, silu_ready, glu_ready, down_done, y_kept, yT_ready, y_added, res_ready = (
            sem(n) for n in ("up_ready", "silu_ready", "glu_ready", "down_done", "y_kept", "yT_ready",
                             "y_added", "res_ready"))

        def tile_rows(s):
            return min(P, 2 * HID - ORDER[s] * P)

        def groups_through(S):
            return GROUPS * (S // STEPS) + S % STEPS // 2 + 1

        block = ctx.enter_context(nc.Block())

        def wait(eng, s, value):
            if isinstance(value, int) and value <= 0:
                return
            eng.wait_ge(s, value)

        def states_loop(eng, body):
            for k in range(K):
                body(k, 0)
                with eng.Fori(1, N // BODY - 1) as i:
                    body(k, i)
                body(k, N // BODY - 1)

        BANK_B, BANK_XP, BANK_C, BANK_Y = 0, 2, 4, 6
        BANKS_DT = (7, 3, 4, 6)
        BANKS_DTR = (5, 1)
        BANK_WARM = 4
        PRM_IN = 16 * 7
        BANK_H, BANK_O = 0, 6

        @block.sync
        def _(sp):
            sp.dma_start(xg[:], x_grp).then_inc(x_in, 16)
            sp.dma_start(xc[:], x_chan).then_inc(xc_in, 16)
            sp.dma_start(w_in[:], in_proj).then_inc(win_in, 16)
            sp.dma_start(w_conv[:], conv_w).then_inc(conv_in, 16)
            sp.dma_start(w_xp[:], xproj).then_inc(prm_in, 16)
            sp.dma_start(b_conv[:], conv_b).then_inc(prm_in, 16)
            sp.dma_start(a_log[:], a_logs).then_inc(prm_in, 16)
            sp.dma_start(dsk[:], d_skip).then_inc(prm_in, 16)
            sp.wait_ge(dt_zero, 1)
            for odd in range(2):
                sp.dma_start(w_dt[odd * R:(odd + 1) * R].rearrange("r (h o) d -> r h o d", o=2)[:, :, odd],
                             dt_wb[0:R].rearrange("r (h o) d -> r h o d", o=2)[:, :, odd]).then_inc(prm_in, 16)
            sp.dma_start(w_dt[2 * R:2 * R + 1], dt_wb[R:R + 1]).then_inc(prm_in, 16)
            sp.dma_start(xt[:], x_tok).then_inc(xt_in, 16)
            sp.dma_start(w_out[:], out_proj).then_inc(out_in, 16)
            sp.dma_start(wqkv[:], w_qkv).then_inc(qkv_in, 16)
            sp.dma_start(w_rt[:], w_router).then_inc(qkv_in, 16)
            def load_raw(pair):
                for half in range(2):
                    sp.dma_start(wraw[half * C:(half + 1) * C, pair % 2],
                                 w_up[:, pair]).then_inc(raw_in[pair % 2], 16)

            def load_down(pair):
                first, second, to = w_down[2 * pair], w_down[2 * pair + 1], wdn[:, pair % 2]
                own = P - CUT
                full = (HID - own) // P
                last = HID - own - full * P
                for dst, src in (
                        (to[:, 0:SHARED, :], first[0:SHARED * P].rearrange("(j p) c -> p j c", p=P)),
                        (to[0:CUT, SHARED, :], first[SHARED * P:HID]),
                        (to[CUT:P, SHARED + 1, :], second[0:own]),
                        (to[:, SHARED + 2:SHARED + 2 + full, :],
                         second[own:own + full * P].rearrange("(j p) c -> p j c", p=P)),
                        (to[0:last, SHARED + 2 + full, :], second[own + full * P:HID])):
                    sp.dma_start(dst, src).then_inc(down_in[pair % 2], 16)

            sp.wait_ge(shared_zero, 1)
            for pair in range(2):
                load_raw(pair)
                load_down(pair)
            for pair in range(2, PAIRS):
                sp.wait_ge(slot_ready[pair % 2], 1)
                load_raw(pair)
            for pair in range(2, PAIRS):
                sp.wait_ge(w_split, pair - 1)
                sp.wait_ge(up_ready, STEPS * (pair - 1))
                sp.dma_start(wup[:, pair % 2].rearrange("p a b h -> p (a b h)").bitcast(FP32),
                             wnext[:, pair % 2].rearrange("p a b h -> p (a b h)").bitcast(FP32)).then_inc(slot_ready[pair % 2], 16)
                sp.wait_ge(down_done, GROUPS * (pair - 1))
                load_down(pair)
            sp.wait_ge(res_ready, 1)
            sp.dma_start(out, res[:]).then_inc(stored, 16)
            sp.wait_ge(stored, 16)

        @block.gpsimd
        def _(pool):
            done = [0]

            def step(ins):
                done[0] += 1
                ins.then_inc(pool_step, 1)

            def wait_steps():
                pool.wait_ge(pool_step, done[0])

            step(nc.gpsimd.memset(sel_grp[:], 0.0))
            step(nc.gpsimd.memset(ident[:], 0.0))
            step(nc.gpsimd.memset(sel_row[:], 0.0))
            step(nc.gpsimd.memset(flip[:], 0.0))
            step(nc.gpsimd.memset(minus[:], 0.0))
            wait_steps()
            step(nc.gpsimd.affine_select(out=sel_grp[:], in_=sel_grp[:], compare_op=ALU.not_equal, fill=1.0,
                                         base=0, pattern=[[-G, B], [-1, G], [0, 2]], channel_multiplier=1))
            step(nc.gpsimd.affine_select(out=ident[:], in_=ident[:], compare_op=ALU.not_equal, fill=1.0,
                                         base=0, pattern=[[-1, P]], channel_multiplier=1))
            step(nc.gpsimd.affine_select(out=flip[:], in_=flip[:], compare_op=ALU.not_equal, fill=1.0,
                                         base=1 - D, pattern=[[1, D]], channel_multiplier=1))
            for part in range(3):
                wait_steps()
                step(nc.gpsimd.affine_select(out=sel_row[:], in_=sel_row[:], compare_op=ALU.not_equal, fill=1.0,
                                             base=-2 * N * part, pattern=[[-1, 2 * N]], channel_multiplier=1))
            wait_steps()
            step(nc.gpsimd.affine_select(out=minus[:], in_=minus[:], compare_op=ALU.not_equal, fill=-1.0,
                                         base=0, pattern=[[0, 2], [-1, 6 * N]], channel_multiplier=1))
            wait_steps()
            step(nc.gpsimd.affine_select(out=minus[:], in_=minus[:], compare_op=ALU.is_ge, fill=0.0,
                                         base=-2 * N, pattern=[[-2 * N, 2], [0, 6 * N]], channel_multiplier=1))
            pool.wait_ge(prm_in, PRM_IN)
            for k in range(K):
                half, odd = k // 2, k % 2
                for col, row in [(0, 2 * R + N * odd), (N, 2 * R + 2 * N + N * odd)]:
                    for copy in range(3):
                        at = col + 2 * N * copy
                        step(nc.gpsimd.tensor_copy(w_rep[:, k, at:at + N], w_xp[:, half, row:row + N]))
            step(nc.gpsimd.memset(band[:], 0.0))
            step(nc.gpsimd.iota(rank[:], pattern=[[-1, E]], base=E, channel_multiplier=0,
                                allow_small_or_imprecise_dtypes=True))
            for sign in (1, -1):
                wait_steps()
                step(nc.gpsimd.affine_select(out=band[:], in_=band[:], compare_op=ALU.is_ge, fill=NEG, base=REACH,
                                             pattern=[[sign * (L - WIN - P), 2], [sign, WIN]], channel_multiplier=-sign))
            step(nc.gpsimd.memset(pr[:], 0.0))
            step(nc.gpsimd.memset(eps[:], 1e-5))

            for k in range(1, K - 1):
                pool.wait_ge(ex_ready, k + 1)
                nc.gpsimd.tensor_scalar(rd[:, k, :], ex[:, k, :], 1.0, -1.0, ALU.add, ALU.add).then_inc(rounding_ready, 1)
                pool.wait_ge(rounding_ready, 2 * k - 1)
                nc.gpsimd.tensor_tensor(rd[:, k, :], ex[:, k, :], rd[:, k, :], ALU.subtract).then_inc(rounding_ready, 1)

            def body(k, i):
                for q in range(BODY):
                    n = k * N + BODY * i + q
                    wait(pool, scanned, n + 1)
                    if q % 2 == 0:
                        wait(pool, c_kept, k * N // 2 + BODY // 2 * i + q // 2 + 1)
                    wait(pool, summed, n - BODY + 1)
                    nc.gpsimd.tensor_tensor(hc[:, q], hs[:, q], cs[:, q], ALU.mult).then_inc(weighted, 1)

            states_loop(nc.gpsimd, body)

            pool.wait_ge(weighted, K * N)
            for pair in range(PAIRS):
                to = wup if pair < 2 else wnext
                pool.wait_ge(raw_in[pair % 2], 32 * (pair // 2 + 1))
                if pair == 2:
                    pool.wait_ge(y_ready, 1)
                if pair >= 2:
                    nc.gpsimd.tensor_copy(to[:, pair % 2], wraw[:, pair % 2]).then_inc(w_rounded, 1)
                pool.wait_ge(w_rounded, pair + 1)
                nc.gpsimd.tensor_tensor(to[C:2 * C, pair % 2], wraw[C:2 * C, pair % 2],
                                        to[C:2 * C, pair % 2].bitcast(FP32), ALU.subtract
                                        ).then_inc(slot_ready[pair] if pair < 2 else w_split, 1)
                if pair < 2:
                    pool.wait_ge(slot_ready[pair], 1)
                else:
                    pool.wait_ge(w_split, pair - 1)

        @block.scalar
        def _(act):
            nc.scalar.preload_act_table_set("sqrt_and_others")
            act.wait_ge(dve_step, 3)
            nc.scalar.activation(sd_g[:], mr_g[:, 1:2], ACT.Sqrt).then_inc(sd_ready, 1)
            nc.scalar.preload_act_table_set("silu_and_others")
            act.wait_ge(xi_ready, 1)
            act.wait_ge(pad_zero, 1)
            for b in range(B):
                last = nc.scalar.activation(xpad[:, b, 1:H + 1, 1:W + 1],
                                            ps[:, 0, b * L:(b + 1) * L].rearrange("p (h w) -> p h w", h=H), ACT.Copy)
                last.then_inc(xi_padded, 1)
            act.wait_ge(xi_ready, 2)
            nc.scalar.activation(zs[:], ps[:, 1, :], ACT.Silu).then_inc(z_done, 1)
            act.wait_ge(prm_in, PRM_IN)
            act.wait_ge(conv_ready, 1)
            nc.scalar.activation(u[:, 0, :], ps[:, 2, :], ACT.Silu, bias=b_conv[:]).then_inc(u_ready, 1)

            def by_columns(ap, inner):
                return ap.rearrange(f"p (b {inner}) -> p b w h", b=B, h=H, w=W)

            nc.scalar.activation(by_columns(u[:, 2, :], "w h"), by_columns(ps[:, 2, :], "h w"), ACT.Silu,
                                 bias=b_conv[:]).then_inc(u_ready, 1)
            nc.scalar.preload_act_table_set("exp_and_others")
            nc.scalar.activation(a_exp[:], a_log[:], ACT.Exp).then_inc(aexp_ready, 1)

            def keep_dtr(half):
                act.wait_ge(dtr_ready, half + 1)
                nc.scalar.activation(dtr[0:2 * R, half, :], ps[0:2 * R, BANKS_DTR[half], :], ACT.Copy).then_inc(dtr_kept, 1)

            def keep_part(k, part):
                if isinstance(part, int) and part == 0:
                    act.wait_ge(proj_ready, k + 1)
                else:
                    act.wait_ge(rest_ready, 2 * k + part)
                nc.scalar.activation(bc[:, k % 2, :], ps[0:6 * N, BANK_XP if k else BANK_B, :], ACT.Copy).then_inc(part_kept, 1)

            def exp_part(k):
                act.wait_ge(abs_ready, k + 1)
                nc.scalar.activation(ex[:, k, :], ex[:, k, :], ACT.Exp, scale=-1.0).then_inc(ex_ready, 1)

            keep_dtr(0)
            keep_part(0, 0)
            keep_dtr(1)
            exp_part(0)
            keep_part(0, 1)
            for k in range(1, K):
                exp_part(k)
                if k == 2:
                    keep_part(0, 2)
            nc.scalar.preload_act_table_set("natural_log")
            for k in range(K):
                act.wait_ge(ex_ready, k + 1)
                nc.scalar.activation(lg[k], ex[:, k, :], ACT.Ln, bias=1.0).then_inc(log_ready, 1)
            act.wait_ge(u_ready, 3)
            nc.scalar.activation(by_columns(u[:, 3, :], "w h"), by_columns(ps[:, BANK_XP, :], "h w"),
                                 ACT.Copy).then_inc(u_ready, 1)
            nc.scalar.preload_act_table_set("exp_and_others")

            def body(k, i):
                if isinstance(i, int) and i == 0:
                    act.wait_ge(delta_ready, k + 1)
                for q in range(BODY):
                    n = k * N + BODY * i + q
                    wait(act, scanned, n - BODY + 1)
                    col = BODY * i + q
                    nc.scalar.activation(da[:, q, :, 1:L],
                                         delta[:, k % 2, :].rearrange("p (b l) -> p b l", b=B)[:, :, 1:L], ACT.Exp,
                                         scale=a_neg[:, bass.ds(k * N + col, 1)]).then_inc(da_ready, 1)
                    if q % 2:
                        g = k * N // 2 + BODY // 2 * i + q // 2
                        two = slice(q - 1, q + 1)
                        act.wait_ge(c_ready, g + 1)
                        wait(act, weighted, k * N + BODY * i + q - BODY + 1)
                        nc.scalar.activation(cs[:, two], ps[:, BANK_C:BANK_C + 2, :], ACT.Copy).then_inc(c_kept, 1)
                    if q == 2 and k + 1 < K and not (isinstance(i, int) and i == N // BODY - 1):
                        keep_part(k + 1, i)

            act.wait_ge(aneg_ready, 1)
            act.wait_ge(da_zero, 1)
            states_loop(nc.scalar, body)

            nc.scalar.preload_act_table_set("sqrt_and_others")
            for pair in range(2):
                act.wait_ge(raw_in[pair], 32)
                nc.scalar.activation(wup[:, pair], wraw[:, pair], ACT.Copy).then_inc(w_rounded, 1)
            act.wait_ge(var_ready, NT)
            nc.scalar.activation(sd[:], mv[:, :, 1], ACT.Sqrt, bias=eps[:]).then_inc(sdt_ready, 1)
            nc.scalar.preload_act_table_set("exp_and_others")
            act.wait_ge(tnT_ready, 2)
            nc.scalar.activation(tnT[0:C, L:T], ps[0:C, 3, 0:L], ACT.Copy).then_inc(tnT_kept, 1)
            act.wait_ge(qk_ready, 1)
            nc.scalar.activation(qT[:], ps[0:C, 0, :], ACT.Copy).then_inc(q_kept, 1)
            act.wait_ge(v_ready, 1)
            nc.scalar.activation(v[:], ps[:, 4, 0:NT * C].rearrange("p (t c) -> p t c", t=NT), ACT.Copy).then_inc(v_kept, 1)
            for t in range(NT):
                act.wait_ge(mx_ready, t // 2 + 1)
                first = (t % 2) * (L - WIN)
                nc.scalar.activation(pr[:, t, first:first + WIN], sc[:, t, :], ACT.Exp, bias=nm[:, t:t + 1], scale=C ** -0.5,
                                     accum_out=sums[:, t:t + 1]).then_inc(pr_ready, 1)
            act.wait_ge(prT_ready, 2)
            nc.scalar.activation(prT[:, 2:4], ps[:, 1, :], ACT.Copy).then_inc(prT_kept_a, 1)
            nc.scalar.preload_act_table_set("sqrt_and_others")
            act.wait_ge(var_ready, 2 * NT)
            nc.scalar.activation(sd[:], mv[:, :, 1], ACT.Sqrt, bias=eps[:]).then_inc(sdt_ready, 1)
            nc.scalar.preload_act_table_set("exp_and_others")
            act.wait_ge(fT_ready, 1)
            nc.scalar.activation(fT[:], ps[0:C, 2, :], ACT.Copy).then_inc(fT_kept, 1)
            act.wait_ge(lsub_ready, 1)
            nc.scalar.activation(le[:], lo[:], ACT.Exp).then_inc(le_ready, 1)

            nc.scalar.preload_act_table_set("silu_and_others")

            def keep_pair(pair):
                act.wait_ge(down_done, GROUPS * (pair + 1))
                wait(act, yT_ready, pair)
                nc.scalar.activation(ysb[:], ps[:, BANK_O + pair % 2, :], ACT.Copy).then_inc(y_kept, 1)

            for pair in range(PAIRS):
                for s in range(STEPS):
                    S = STEPS * pair + s
                    rows = tile_rows(s)
                    act.wait_ge(up_ready, S + 1)
                    wait(act, glu_ready, S - 1)
                    nc.scalar.activation(si[0:rows, S % 2, :], ps[0:rows, BANK_H + 2 * (S % 3), :],
                                         ACT.Silu).then_inc(silu_ready, 1)
                    if pair and s == 3:
                        keep_pair(pair - 1)
            keep_pair(PAIRS - 1)

        @block.vector
        def _(dve):
            done = [0]

            def chain(ins):
                done[0] += 1
                ins.then_inc(dve_step, 1)
                dve.wait_ge(dve_step, done[0])

            nc.vector.memset(gl[:, 0, 0:T // 2], 0.0).then_inc(warm_set, 1)
            nc.vector.memset(w_dt[0:2 * R], 0.0).then_inc(dt_zero, 1)
            nc.vector.memset(xpad[:], 0.0).then_inc(pad_zero, 1)
            dve.wait_ge(x_in, 16)
            chain(nc.vector.bn_stats(st_g[:], xg[:]))
            chain(nc.vector.bn_aggr(mr_g[:], st_g[:]))
            chain(nc.vector.tensor_scalar(mr_g[:, 1:2], mr_g[:, 1:2], 1e-5, None, ALU.add))
            dve.wait_ge(sd_ready, 1)
            nc.vector.reciprocal(mr_g[:, 1:2], sd_g[:]).then_inc(mr_ready, 1)
            dve.wait_ge(mrc_ready, 1)
            nc.vector.tensor_copy(mr_c[:], ps[0:C, 7, 0:2 * B].rearrange("p (b s) -> p b s", b=B)).then_inc(mrc_copied, 1)
            dve.wait_ge(mrc_copied, 1)
            dve.wait_ge(xc_in, 16)
            for b in range(B):
                last = nc.vector.tensor_scalar(xn[:, b * L:(b + 1) * L], xc[:, b * L:(b + 1) * L], mr_c[:, b, 0:1],
                                               mr_c[:, b, 1:2], ALU.subtract, ALU.mult)
                last.then_inc(xn_ready, 1)
            nc.vector.memset(wdn[:, :, SHARED:SHARED + 2, :], 0.0).then_inc(shared_zero, 1)
            nc.vector.memset(dtr[2 * R:2 * R + 1], 1.0).then_inc(dtr_set, 1)
            nc.vector.memset(da[:, :, :, 0:1], 0.0).then_inc(da_zero, 1)
            nc.vector.memset(tnT[C:C + 1, :], 1.0).then_inc(tnT_kept, 1)
            dve.wait_ge(prm_in, PRM_IN)
            dve.wait_ge(pool_step, 8)
            for half in range(K // 2):
                chain(nc.vector.tensor_scalar(d_cross[:, half, :], ident[:], dsk[:, 2 * half:2 * half + 1], None, ALU.mult))
                nc.vector.scalar_tensor_tensor(d_cross[:, half, :], flip[:], dsk[:, 2 * half + 1:2 * half + 2],
                                               d_cross[:, half, :], ALU.mult, ALU.add).then_inc(diag_ready, 1)
            dve.wait_ge(aexp_ready, 1)
            nc.vector.tensor_scalar(a_neg[:], a_exp[:], -1.0, None, ALU.mult).then_inc(aneg_ready, 1)

            def step(ins):
                done[0] += 1
                ins.then_inc(dve_step, 1)
                return done[0]

            def prepare(k, part, marks):
                rounding = rd[:, k % 3, :]
                if part == 0 and k in BY_VECTOR:
                    dve.wait_ge(ex_ready, k + 1)
                    marks["e"] = step(nc.vector.tensor_scalar(rounding, ex[:, k, :], 1.0, -1.0, ALU.add, ALU.add))
                elif part == 1 and k in BY_VECTOR:
                    dve.wait_ge(dve_step, marks["e"])
                    marks["rounding"] = step(nc.vector.tensor_tensor(rounding, ex[:, k, :], rounding, ALU.subtract))
                elif part == 2:
                    if k in BY_VECTOR:
                        dve.wait_ge(dve_step, marks["rounding"])
                    else:
                        dve.wait_ge(rounding_ready, 2 * k)
                    if k in above:
                        dve.wait_ge(above_kept, 2)
                        all_but_ln = nc.vector.tensor_tensor(rounding, above[k], rounding, ALU.add)
                    else:
                        all_but_ln = nc.vector.scalar_tensor_tensor(rounding, ps[:, BANKS_DT[k], :], 0.0, rounding,
                                                                    ALU.max, ALU.add)
                    marks["all but ln"] = step(all_but_ln)
                elif part == 3:
                    dve.wait_ge(dve_step, marks["all but ln"])
                    dve.wait_ge(log_ready, k + 1)
                    nc.vector.tensor_tensor(delta[:, k % 2, :], rounding, lg[k], ALU.add).then_inc(delta_ready, 1)
                    dve.wait_ge(delta_ready, k + 1)
                    dve.wait_ge(u_ready, K if k else 1)
                    nc.vector.tensor_tensor(du[:, k % 2, :], delta[:, k % 2, :], u[:, k, :], ALU.mult).then_inc(du_ready, 1)

            def body(k, i):
                marks = {} if isinstance(i, int) and i == 0 and k + 1 < K else None
                if isinstance(i, int) and i == 0:
                    dve.wait_ge(du_ready, k + 1)

                def times_b(q):
                    n = k * N + BODY * i + q
                    dve.wait_ge(b_ready, n + 1)
                    wait(dve, scanned, n - 1)
                    nc.vector.tensor_tensor(bdu[:, q % 2, :], ps[:, BANK_B + q % 2, :], du[:, k % 2, :],
                                            ALU.mult).then_inc(b_used, 1)

                def scan(q):
                    n = k * N + BODY * i + q
                    dve.wait_ge(da_ready, n + 1)
                    dve.wait_ge(b_used, n + 1)
                    wait(dve, weighted, n - BODY + 1)
                    nc.vector.tensor_tensor_scan(hs[:, q, :], da[:, q].rearrange("p b l -> p (b l)"),
                                                 bdu[:, q % 2, :], 0.0, ALU.mult, ALU.add).then_inc(scanned, 1)

                times_b(0)
                for q in range(1, BODY):
                    times_b(q)
                    scan(q - 1)
                    if marks is not None:
                        prepare(k + 1, q - 1, marks)
                if marks is not None:
                    prepare(k + 1, BODY - 1, marks)
                scan(BODY - 1)

            for k in range(K):
                dve.wait_ge(dt_ready, k + 1)
                nc.vector.tensor_scalar(ex[:, k, :].bitcast(mybir.dt.int32),
                                        ps[:, BANKS_DT[k], :].bitcast(mybir.dt.int32), 0x7FFFFFFF, None,
                                        ALU.bitwise_and).then_inc(abs_ready, 1)

            def keep_above(k):
                nc.vector.tensor_scalar(above[k], ps[:, BANKS_DT[k], :], 0.0, None, ALU.max).then_inc(above_kept, 1)

            keep_above(3)
            first_marks = {}
            for part in range(BODY):
                prepare(0, part, first_marks)
                if part == 2:
                    keep_above(2)
                    dve.wait_ge(flip_ready, 1)
                    nc.vector.tensor_copy(u[:, 1, :], ps[:, BANK_XP, :]).then_inc(u_ready, 1)
            states_loop(nc.vector, body)

            dve.wait_ge(y_ready, 1)
            dve.wait_ge(z_done, 1)
            for b in range(B):
                one = slice(b * L, (b + 1) * L)
                nc.vector.tensor_tensor(yg[:, one], ps[:, BANK_Y, one], zs[:, one], ALU.mult).then_inc(yg_ready, 1)
            dve.wait_ge(op_ready, 1)
            dve.wait_ge(xt_in, 16)

            def over(ap, n):
                return ap.unsqueeze(2).broadcast_to([P, NT, n])

            def layer_norm(src, turn):
                for t in range(NT):
                    last = step(nc.vector.bn_stats(st[:, t, :], src[:, t, :]))
                dve.wait_ge(dve_step, last)
                for t in range(NT):
                    aggregated = nc.vector.bn_aggr(mv[:, t, :], st[:, t, :])
                    aggregated.then_inc(var_ready, 1)
                dve.wait_ge(var_ready, NT * turn)
                chain(nc.vector.tensor_tensor(dm[:], src[:], over(mv[:, :, 0], C), ALU.subtract))
                dve.wait_ge(sdt_ready, turn)
                chain(nc.vector.reciprocal(rs[:], sd[:]))
                for b in range(B):
                    two = slice(2 * b, 2 * b + 2)
                    if turn == 1:
                        normed = nc.vector.tensor_tensor(tn[:, two], dm[:, two], rs[:, two].unsqueeze(2).broadcast_to([P, 2, C]),
                                                         ALU.mult)
                    else:
                        normed = nc.vector.tensor_tensor(
                            tn2[:, two], dm[:, two].unsqueeze(2).broadcast_to([P, 2, 2, C]),
                            rs[:, two].unsqueeze(2).unsqueeze(3).broadcast_to([P, 2, 2, C]), ALU.mult)
                    normed.then_inc(tn_ready, 1)

            chain(nc.vector.tensor_tensor(t1[:], xt[:], ps[:, 0, 0:NT * C].rearrange("p (t c) -> p t c", t=NT), ALU.add))
            layer_norm(t1, 1)
            dve.wait_ge(tnT_ready, 1)
            nc.vector.tensor_copy(tnT[0:C, 0:L], ps[0:C, 1, 0:L]).then_inc(tnT_kept, 1)
            dve.wait_ge(qk_ready, 2)
            for b in range(B):
                nc.vector.tensor_copy(kT[:, b * L:(b + 1) * L], ps[0:C, 2, b * L:(b + 1) * L]).then_inc(k_kept, 1)
            for b in range(B):
                two = slice(2 * b, 2 * b + 2)
                dve.wait_ge(s_ready, b + 1)
                chain(nc.vector.tensor_tensor(sc[:, two, :],
                                              ps[:, 5 + b, 0:2 * WIN].rearrange("p (t l) -> p t l", t=2), band[:], ALU.add))
                chain(nc.vector.tensor_reduce(mx[:, two], sc[:, two, :], AX.X, ALU.max))
                nc.vector.tensor_scalar(nm[:, two], mx[:, two], -(C ** -0.5), None, ALU.mult).then_inc(mx_ready, 1)
            dve.wait_ge(prT_ready, 1)
            nc.vector.tensor_copy(prT[:, 0:2], ps[:, 0, :].rearrange("p (t k q) -> p t k q", t=2, k=2)).then_inc(prT_kept_d, 1)
            dve.wait_ge(pr_ready, NT)
            chain(nc.vector.reciprocal(rsum[:], sums[:]))
            dve.wait_ge(o_ready, 1)
            chain(nc.vector.tensor_tensor(ov[:], ps[:, 7, 0:NT * C].rearrange("p (t c) -> p t c", t=NT), over(rsum[:], C), ALU.mult))
            chain(nc.vector.tensor_tensor(t2[:], t1[:], ov[:], ALU.add))
            layer_norm(t2, 2)
            nc.vector.tensor_copy(acc[:, :, 0, :], t2[:]).then_inc(acc_set, 1)
            nc.vector.memset(acc[:, :, 1, :], 0.0).then_inc(acc_set, 1)
            dve.wait_ge(fT_ready, 1)
            dve.wait_ge(fT_kept, 1)
            nc.vector.tensor_copy(fh[:], ps[:, 2, :]).then_inc(f_split, 1)
            dve.wait_ge(f_split, 1)
            nc.vector.tensor_tensor(fl[:], ps[:, 2, :], fh[:].bitcast(FP32), ALU.subtract).then_inc(f_split, 1)

            dve.wait_ge(lo_ready, NT)
            lps = ps[:, 7, 0:NT * E].rearrange("p (t e) -> p t e", t=NT)
            chain(nc.vector.tensor_reduce(g1[:], lps, AX.X, ALU.max))
            nc.vector.tensor_tensor(lo[:], lps, over(g1[:], E), ALU.subtract).then_inc(lsub_ready, 1)
            ranks = rank[:].unsqueeze(1).broadcast_to([P, NT, E])

            def softmax():
                dve.wait_ge(le_ready, 1)
                chain(nc.vector.tensor_reduce(g2[:], le[:], AX.X, ALU.add))
                chain(nc.vector.reciprocal(g3[:], g2[:]))
                chain(nc.vector.tensor_tensor(pb[:], le[:], over(g3[:], E), ALU.mult))

            def largest(src, top):
                chain(nc.vector.tensor_reduce(top[:], src[:], AX.X, ALU.max))
                chain(nc.vector.tensor_tensor(key[:], src[:], over(top[:], E), ALU.is_equal))
                chain(nc.vector.tensor_tensor(key[:], key[:], ranks, ALU.mult))

            def lowest_index(one_hot):
                chain(nc.vector.tensor_reduce(g1[:], key[:], AX.X, ALU.max))
                chain(nc.vector.tensor_tensor(one_hot[:], key[:], over(g1[:], E), ALU.is_equal))

            def renorm():
                chain(nc.vector.tensor_tensor(g2[:], m1[:], m2[:], ALU.add))
                chain(nc.vector.tensor_scalar(g2[:], g2[:], 1e-9, None, ALU.add))
                chain(nc.vector.reciprocal(g3[:], g2[:]))

            def gate_step(s):
                if s == 0:
                    softmax()
                elif s == 1:
                    largest(pb, m1)
                elif s == 2:
                    lowest_index(oh1)
                    chain(nc.vector.scalar_tensor_tensor(pb2[:], oh1[:], -4.0, pb[:], ALU.mult, ALU.add))
                elif s == 3:
                    largest(pb2, m2)
                elif s == 4:
                    lowest_index(oh2)
                    chain(nc.vector.tensor_tensor(oh1[:], oh1[:], oh2[:], ALU.add))
                elif s == 5:
                    renorm()
                elif s == 6:
                    chain(nc.vector.tensor_tensor(pb[:], pb[:], over(g3[:], E), ALU.mult))
                    chain(nc.vector.tensor_tensor(gate[:], oh1[:], pb[:], ALU.mult))

            def add_pair(pair):
                dve.wait_ge(yT_ready, pair + 1)
                g_ap = gate[:, :, 2 * pair:2 * pair + 2].unsqueeze(3).broadcast_to([P, NT, 2, C])
                nc.vector.tensor_tensor(gy[:], ps[:, BANK_O + pair % 2, :].rearrange("p (t e c) -> p t e c", t=NT, e=2),
                                        g_ap, ALU.mult).then_inc(y_added, 1)
                dve.wait_ge(y_added, 2 * pair + 1)
                if pair < PAIRS - 1:
                    nc.vector.tensor_tensor(acc[:], acc[:], gy[:], ALU.add).then_inc(y_added, 1)
                    dve.wait_ge(y_added, 2 * pair + 2)

            dve.wait_ge(acc_set, 2)
            for pair in range(PAIRS):
                for s in range(STEPS):
                    S = STEPS * pair + s
                    rows = tile_rows(s)
                    dve.wait_ge(silu_ready, S + 1)
                    if S >= 4:
                        dve.wait_ge(down_done, groups_through(S - 4))
                    nc.vector.tensor_tensor(gl[0:rows, S % 4, :], ps[0:rows, BANK_H + 2 * (S % 3) + 1, :],
                                            si[0:rows, S % 2, :], ALU.mult).then_inc(glu_ready, 1)
                    if pair == 0:
                        gate_step(s)
                    elif s == 5:
                        add_pair(pair - 1)
            chain(nc.vector.tensor_tensor(t1[:], acc[:, :, 0, :], acc[:, :, 1, :], ALU.add))
            add_pair(PAIRS - 1)
            chain(nc.vector.tensor_tensor(t2[:], gy[:, :, 0, :], gy[:, :, 1, :], ALU.add))
            nc.vector.tensor_tensor(res[:], t1[:], t2[:], ALU.add).then_inc(res_ready, 1)

        @block.tensor
        def _(pe):
            def keep_warm(count, bank=BANK_WARM):
                for _ in range(count):
                    nc.tensor.matmul(ps[:, bank, :], warm[:, 0:P], warm[:], start=True, stop=True)

            pe.wait_ge(warm_set, 1)
            keep_warm(WARM_UP)
            pe.wait_ge(mr_ready, 1)
            pe.wait_ge(pool_step, 6)
            for b in range(B):
                last = nc.tensor.matmul(ps[0:C, 7, 2 * b:2 * b + 2], sel_grp[:, b].rearrange("p g c -> p (g c)"),
                                        mr_g[:], start=True, stop=True)
            last.then_inc(mrc_ready, 1)
            keep_warm(2)
            pe.wait_ge(xn_ready, B)
            pe.wait_ge(win_in, 16)
            for half in range(2):
                nc.tensor.matmul(ps[:, half, :], w_in[:, half * D:(half + 1) * D], xn[:], start=True,
                                 stop=True).then_inc(xi_ready, 1)
            pe.wait_ge(xi_padded, B)
            pe.wait_ge(conv_in, 16)
            for tap in range(TAPS):
                last = nc.tensor.matmul(ps[:, 2, :], w_conv[:, tap, :],
                                        xpad[:, :, tap // 3:tap // 3 + H, tap % 3:tap % 3 + W],
                                        start=(tap == 0), stop=(tap == TAPS - 1))
            last.then_inc(conv_ready, 1)

            def dt_rows(half):
                nc.tensor.matmul(ps[0:2 * R, BANKS_DTR[half], :], w_xp[:, half, 0:2 * R], u[:, 2 * half, :], start=True,
                                 stop=True).then_inc(dtr_ready, 1)

            def project(k):
                nc.tensor.matmul(ps[0:6 * N, BANK_XP if k else BANK_B, :], w_rep[:, k, :], u[:, 2 * (k // 2), :], start=True,
                                 stop=True).then_inc(proj_ready, 1)

            def take_off(k, part):
                pe.wait_ge(part_kept, 3 * k + part)
                nc.tensor.matmul(ps[0:6 * N, BANK_XP if k else BANK_B, :], minus[:, bass.ds(6 * N * part - 6 * N, 6 * N)],
                                 bc[:, k % 2, :], start=False, stop=True, skip_group_check=True).then_inc(rest_ready, 1)

            def dt_product(k):
                nc.tensor.matmul(ps[:, BANKS_DT[k], :], w_dt[:, k, :], dtr[:, k // 2, :], start=True,
                                 stop=True).then_inc(dt_ready, 1)

            def skip(half):
                nc.tensor.matmul(ps[:, BANK_Y, :], d_cross[:, half, :], u[:, 2 * half, :], start=(half == 0), stop=False)

            def sum_state(q, n):
                wait(pe, weighted, n + 1)
                last_state = isinstance(n, int) and n == K * N - 1
                nc.tensor.matmul(ps[:, BANK_Y, :], ident[:], hc[:, q % BODY, :], start=False,
                                 stop=last_state).then_inc(y_ready if last_state else summed, 1)

            def body(k, i):
                peeled = i if isinstance(i, int) else None
                if peeled == 0:
                    pe.wait_ge(part_kept, 3 * (k + 1))
                for q in range(BODY):
                    n = k * N + BODY * i + q
                    wait(pe, b_used, n - 1)
                    nc.tensor.matmul(ps[:, BANK_B + q % 2, :],
                                     sel_row[:, bass.ds(BODY * i + q, 1)].broadcast_to([6 * N, D]),
                                     bc[:, k % 2, :], start=True, stop=True).then_inc(b_ready, 1)
                    if q % 2 == 0:
                        wait(pe, c_kept, k * N // 2 + BODY // 2 * i + q // 2)
                        for p in (q, q + 1):
                            last = nc.tensor.matmul(ps[:, BANK_C + p % 2, :],
                                                    sel_row[:, bass.ds(N + BODY * i + p, 1)].broadcast_to([6 * N, D]),
                                                    bc[:, k % 2, :], start=True, stop=True)
                        last.then_inc(c_ready, 1)
                    if not (isinstance(n, int) and n < LAG):
                        sum_state(q - LAG, n - LAG)
                    if q == 1 and k + 1 < K:
                        if peeled == 0:
                            if k == 0:
                                pe.wait_ge(delta_ready, 1)
                                keep_warm(5, BANKS_DT[0])
                                pe.wait_ge(u_ready, K)
                            project(k + 1)
                        elif peeled is None:
                            take_off(k + 1, i)

            pe.wait_ge(u_ready, 1)
            pe.wait_ge(prm_in, PRM_IN)
            dt_rows(0)
            pe.wait_ge(pool_step, 13 + 6 * K)
            project(0)
            pe.wait_ge(u_ready, 2)
            pe.wait_ge(z_done, 1)
            dt_rows(1)
            pe.wait_ge(dtr_kept, 1)
            pe.wait_ge(dtr_set, 1)
            pe.wait_ge(mrc_copied, 1)
            dt_product(0)
            dt_product(1)
            pe.wait_ge(dtr_kept, 2)
            dt_product(2)
            take_off(0, 1)
            dt_product(3)
            take_off(0, 2)
            pe.wait_ge(diag_ready, K // 2)
            nc.tensor.matmul(ps[:, BANK_XP, :], flip[:], u[:, 0, :], start=True, stop=True).then_inc(flip_ready, 1)
            pe.wait_ge(above_kept, 1)
            skip(0)
            skip(1)
            pe.wait_ge(above_kept, 2)
            states_loop(nc.tensor, body)
            for n in range(K * N - LAG, K * N):
                sum_state(n, n)

            keep_warm(3)
            pe.wait_ge(out_in, 16)
            for t in range(NT):
                pe.wait_ge(yg_ready, t // 2 + 1)
                last = nc.tensor.matmul(ps[:, 0, t * C:(t + 1) * C], yg[:, t * P:(t + 1) * P], w_out[:], start=True, stop=True)
            last.then_inc(op_ready, 1)

            keep_warm(12)
            for t in range(NT):
                pe.wait_ge(tn_ready, t // 2 + 1)
                last = nc.tensor.matmul(ps[0:C, 1 + 2 * (t // 2), (t % 2) * P:(t % 2 + 1) * P], tn[:, t, :], ident[:],
                                        start=True, stop=True)
                if t % 2:
                    last.then_inc(tnT_ready, 1)
            keep_warm(2)
            pe.wait_ge(tnT_kept, 3)
            pe.wait_ge(qkv_in, 32)
            for j in range(2):
                nc.tensor.matmul(ps[0:C, 2 * j, :], wqkv[:, j, :], tnT[:], start=True, stop=True).then_inc(qk_ready, 1)
            for t in range(NT):
                last = nc.tensor.matmul(ps[:, 4, t * C:(t + 1) * C], tnT[:, t * P:(t + 1) * P], wqkv[:, 2, :], start=True, stop=True)
            last.then_inc(v_ready, 1)
            pe.wait_ge(q_kept, 1)
            for b in range(B):
                pe.wait_ge(k_kept, b + 1)
                for t in (2 * b, 2 * b + 1):
                    last = nc.tensor.matmul(ps[:, 5 + b, (t % 2) * WIN:(t % 2 + 1) * WIN], qT[:, t * P:(t + 1) * P],
                                            kT[:, b * L + (t % 2) * (L - WIN):b * L + (t % 2) * (L - WIN) + WIN], start=True, stop=True)
                last.then_inc(s_ready, 1)
            pe.wait_ge(v_kept, 1)
            keep_warm(8)
            for t in range(NT):
                pe.wait_ge(pr_ready, t + 1)
                for kt in range(2):
                    at = ((t % 2) * 2 + kt) * P
                    last = nc.tensor.transpose(ps[:, t // 2, at:at + P], pr[:, t, kt * P:(kt + 1) * P], ident[:])
                if t % 2:
                    last.then_inc(prT_ready, 1)
            for t in range(NT):
                if t < 2:
                    pe.wait_ge(prT_kept_d, 1)
                else:
                    pe.wait_ge(prT_kept_a, 1)
                for kt in range(2):
                    last = nc.tensor.matmul(ps[:, 7, t * C:(t + 1) * C], prT[:, t, kt, :], v[:, 2 * (t // 2) + kt, :],
                                            start=(kt == 0), stop=(kt == 1))
            last.then_inc(o_ready, 1)

            keep_warm(16)
            for t in range(NT):
                pe.wait_ge(tn_ready, B + t // 2 + 1)
                last = nc.tensor.transpose(ps[:, 2, t * P:(t + 1) * P],
                                           tn2[:, t].rearrange("p a c -> p (a c)"), ident[:])
            last.then_inc(fT_ready, 1)
            keep_warm(4)
            pe.wait_ge(fT_kept, 1)
            for t in range(NT):
                nc.tensor.matmul(ps[:, 7, t * E:(t + 1) * E], fT[0:C, t * P:(t + 1) * P], w_rt[:], start=True,
                                 stop=True).then_inc(lo_ready, 1)

            def ups(pair, s):
                S = STEPS * pair + s
                rows, at = tile_rows(s), ORDER[s] * P
                wait(pe, glu_ready, S - 2)
                for part, rest in ((fh, False), (fl, True)):
                    if S == 0:
                        pe.wait_ge(f_split, 1 + rest)
                    for which in range(2):
                        weights = wup[:, pair % 2, which].rearrange("p e h -> p (e h)")
                        last = nc.tensor.matmul(ps[0:rows, BANK_H + 2 * (S % 3) + which, :],
                                                weights[:, at:at + rows], part[:],
                                                start=not rest, stop=rest)
                last.then_inc(up_ready, 1)

            def downs(pair, j):
                pe.wait_ge(glu_ready, STEPS * pair + min(2 * j + 2, STEPS))
                if j == 0:
                    pe.wait_ge(down_in[pair % 2], 16 * 5 * (pair // 2 + 1))
                    wait(pe, y_added, 2 * (pair - 2) + 1)
                    pe.wait_ge(lsub_ready, 1)
                for e in range(2):
                    s = min(2 * j + e, STEPS - 1)
                    rows = tile_rows(s)
                    tile = SHARED + e if s == STEPS - 1 else ORDER[s] + e
                    last = nc.tensor.matmul(ps[e * C:(e + 1) * C, BANK_O + pair % 2, :], wdn[0:rows, pair % 2, tile, :],
                                            gl[0:rows, (STEPS * pair + s) % 4, :], start=(j == 0), stop=(j == GROUPS - 1))
                last.then_inc(down_done, 1)

            def turn_pair(pair):
                pe.wait_ge(y_kept, pair + 1)
                for t in range(NT):
                    last = nc.tensor.transpose(ps[:, BANK_O + pair % 2, t * P:(t + 1) * P], ysb[:, t * P:(t + 1) * P],
                                               ident[:])
                last.then_inc(yT_ready, 1)

            for pair in range(PAIRS):
                pe.wait_ge(slot_ready[pair % 2], 1 + 16 * (pair // 2))
                for s in range(STEPS):
                    ups(pair, s)
                    if s >= 3 and s % 2:
                        downs(pair, (s - 3) // 2)
                    if pair and s < 2:
                        downs(pair - 1, GROUPS - 2 + s)
                    if pair and s == 4:
                        turn_pair(pair - 1)
            downs(PAIRS - 1, GROUPS - 2)
            downs(PAIRS - 1, GROUPS - 1)
            turn_pair(PAIRS - 1)


def kernel(**inputs):
    import numpy as _np
    import concourse.bacc as _bacc
    from concourse import mybir as _mybir
    from concourse.bass_utils import run_bass_kernel_spmd as _run

    i = {n: _np.asarray(a) for n, a in inputs.items()}
    x = i["x"]
    tok = x.reshape(T, C)
    cw = i["L0_conv_conv_w"]
    laid = {
        "x_grp": x.reshape(B, L, G, 2).transpose(0, 2, 3, 1).reshape(B * G, 2 * L),
        "x_chan": tok.T,
        "x_tok": tok.reshape(NT, P, C).transpose(1, 0, 2),
        "in_proj": i["L0_conv_in_proj_w"],
        "conv_w": cw.transpose(1, 2, 3, 0).reshape(D, TAPS, D),
        "conv_b": i["L0_conv_conv_b"].reshape(D, 1),
        "xproj": i["L0_conv_xproj_w"].T.reshape(D, K // 2, 2 * R + 4 * N),
        "dt_wb": _np.concatenate([i["L0_conv_dt_w"].transpose(2, 0, 1), i["L0_conv_dt_b"][None]], axis=0),
        "a_logs": i["L0_conv_A_logs"].transpose(1, 0, 2).reshape(D, K * N),
        "d_skip": _np.stack([d[::-1] if k % 2 else d for k, d in enumerate(i["L0_conv_Ds"])], axis=1),
        "out_proj": i["L0_conv_out_proj_w"],
        "w_qkv": _np.stack([_np.concatenate([i[f"L1_attn_W{n}"].T, i[f"L1_attn_b{n}"][None]], axis=0) for n in "qkv"], axis=1),
        "w_router": i["L1_ffn_router_w"].T,
        "w_up": _np.stack([i[f"L1_ffn_{n}"].reshape(PAIRS, 2, HID, C).transpose(3, 0, 1, 2) for n in ("w1", "w3")], axis=2),
        "w_down": i["L1_ffn_w2"].transpose(0, 2, 1),
    }
    nc = _bacc.Bacc("TRN2", target_bir_lowering=False, num_devices=1)
    arrays, args = {}, []
    for name, a in laid.items():
        a = _np.ascontiguousarray(a)
        arrays[f"{name}_dram"] = a
        args.append(nc.dram_tensor(f"{name}_dram", a.shape, _mybir.dt.from_np(a.dtype), kind="ExternalInput").ap())
    args.append(nc.dram_tensor("out_dram", (P, NT, C), _mybir.dt.float32, kind="ExternalOutput").ap())
    hybrid_kernel(nc, *args)
    r = _run(nc, [arrays], core_ids=[0])
    return _np.asarray(r.results[0]["out_dram"]).transpose(1, 0, 2).reshape(B, H, W, C)
```
